# Optimizing a Trainium2 kernel written in Bass

```python
import numpy as np
import jax
import jax.numpy as jnp

def _softmax(x, axis=-1):
    return jax.nn.softmax(x, axis=axis)

def _gelu(x):
    return jax.nn.gelu(x, approximate=True)

def _silu(x):
    return jax.nn.silu(x)

def _sigmoid(x):
    return jax.nn.sigmoid(x)

def _layernorm(x, axis=-1, eps=1e-05):
    m = jnp.mean(x, axis=axis, keepdims=True)
    v = jnp.var(x, axis=axis, keepdims=True)
    return (x - m) / jnp.sqrt(v + eps)

def _scatter_add(tgt, idx, src, axis=0):
    return tgt.at[idx].add(src)

def _segment_sum(src, seg, n):
    return jax.ops.segment_sum(src, seg, n)
kernel_name = 'mk_adj_resnorm_d1_adj_r2_fb550d'

def setup_inputs(seed: int=0):
    np.random.seed(seed)
    _w = jnp.asarray

    def _rec_inputs():
        import jax
        import jax.numpy as jnp
        _gk = jax.random.key(seed)
        x = 7.22e-05 + 1 * jax.random.normal(jax.random.fold_in(_gk, 1), (2048, 512), jnp.float32)
        _w = (1.0 + jnp.arange(2048, dtype=jnp.float32)) ** (-0.5)
        _w = _w / _w.mean()
        _pij = jnp.clip(0.000976562 * _w[:, None] * _w[None, :], 0.0, 1.0)
        _a = jax.random.uniform(jax.random.fold_in(_gk, 2), (2048, 2048)) < _pij
        _a = jnp.logical_or(_a, jnp.swapaxes(_a, -1, -2))
        _a = jnp.logical_or(_a, jnp.eye(2048, dtype=bool))
        _af = _a.astype(jnp.float32)
        _d = jnp.maximum(_af.sum(-1), 1.0) ** (-0.5)
        _af = _af * _d[..., :, None] * _d[..., None, :]
        adj = _af
        return (x, adj)
    x, adj = _rec_inputs()

    def _L0_gnn_setup():
        import jax, jax.numpy as jnp
        import numpy as np
        N = 4096
        D = 512

        def adjacent_mat(adj):
            adj = adj + jnp.eye(adj.shape[0], dtype=adj.dtype)
            deg = jnp.sum(adj, axis=1)
            dinv = jnp.where(deg > 0, deg ** (-0.5), 0.0).astype(adj.dtype)
            return dinv[:, None] * adj * dinv[None, :]
        key = jax.random.key(seed)
        k1, k2 = jax.random.split(key)
        x = jax.random.normal(k1, (N, D), dtype=jnp.float32)
        Coefficient2 = 1e-08 * jnp.ones((N, N), dtype=jnp.float32)
        A = jax.random.uniform(k2, (N, N), dtype=jnp.float32)
        return {'x': x, 'Coefficient2': Coefficient2, 'A': A}
    _L0_gnn_all = _L0_gnn_setup()
    _L0_gnn_in = {k: v for k, v in _L0_gnn_all.items() if k in ()}
    del _L0_gnn_all
    return {'x': x, 'adj': adj}

def reference(x, adj):
    import jax
    import jax.numpy as jnp

    def _L0_gnn_ref(x, Coefficient2, A):
        import jax, jax.numpy as jnp
        import numpy as np
        N = 4096
        D = 512

        def adjacent_mat(adj):
            adj = adj + jnp.eye(adj.shape[0], dtype=adj.dtype)
            deg = jnp.sum(adj, axis=1)
            dinv = jnp.where(deg > 0, deg ** (-0.5), 0.0).astype(adj.dtype)
            return dinv[:, None] * adj * dinv[None, :]
        A_c = jax.lax.stop_gradient(A)
        adj = adjacent_mat((A_c + A_c.T) * 0.5)
        y = Coefficient2 @ adj
        y = y @ x
        return y
    x = _layernorm(x + _L0_gnn_ref(x, adj, adj), axis=-1)
    return x

_drawn_inputs = setup_inputs


def setup_inputs(seed=0):
    import zlib

    import numpy as np

    out = dict(_drawn_inputs(seed))
    spreads = {}
    factors = {}
    for name, (base, spread) in spreads.items():
        noise = np.random.default_rng([zlib.crc32(name.encode()), seed]).standard_normal(out[name].shape)
        drawn = base * np.exp(spread * noise) if base else spread * noise
        out[name] = jnp.asarray(drawn.astype(out[name].dtype))
    for name, factor in factors.items():
        out[name] = (out[name] * factor).astype(out[name].dtype)
    return out
```

```python
def build(nc, x, adj, out):
    from contextlib import ExitStack

    import concourse.bass as bass
    from concourse import mybir

    F32, F32R, BF16 = mybir.dt.float32, mybir.dt.float32r, mybir.dt.bfloat16
    ALU = mybir.AluOpType
    ACT = mybir.ActivationFunctionType
    AX = mybir.AxisListType

    P = 128
    N, D = x.shape
    NB = N // P
    HALF = 2
    CB = NB // HALF
    EPS = 1e-5
    TINY = 1e-30
    RING = 4
    XG = 4
    F = 4

    a_rows = adj.rearrange("(b p) n -> b p n", p=P)
    a_cols = adj.rearrange("(k p) (m c) -> m p k c", p=P, c=P)
    x_blocks = x.rearrange("(k p) d -> p k d", p=P)
    x_rows = x.rearrange("(b p) d -> b p d", p=P)
    out_rows = out.rearrange("(b p) d -> b p d", p=P)
    at_scratch = nc.dram_tensor("at_scratch", [NB, P, NB, P], F32).ap()

    ctx = ExitStack()
    with ctx:
        place = [16640]

        def at(name, shape, dt, offset):
            return nc.alloc_sbuf_tensor_at(name, shape, dt, offset=offset)

        def sb(name, shape, dt, size):
            offset = place[0]
            size = -(-size // 32) * 32
            place[0] += size
            return at(name, shape, dt, offset), offset

        def sem(name):
            return ctx.enter_context(nc.semaphore(name))

        u_hi, _ = sb("u_hi", [P, NB, D], F32R, NB * D * F)
        u_lo, u_lo_at = sb("u_lo", [P, NB, D], F32R, NB * D * F)
        x_in = at("x_in", [P, NB, D], F32, u_lo_at)
        z_hi, z_hi_at = sb("z_hi", [P, NB, D], F32R, NB * D * F)
        z_lo, z_lo_at = sb("z_lo", [P, NB, D], F32R, NB * D * F)
        row_ring = at("row_ring", [P, RING, NB, P], F32, z_hi_at)
        junk = at("junk", [P, 2, NB, P], BF16, z_lo_at)
        w_hi, _ = sb("w_hi", [P, 2, NB, P], F32R, 2 * NB * P * F)
        w_lo, _ = sb("w_lo", [P, 2, NB, P], F32R, 2 * NB * P * F)
        rows, _ = sb("rows", [P, 2, NB, P], F32, 2 * NB * P * F)
        cols, _ = sb("cols", [P, 2, NB, P], F32, 2 * NB * P * F)
        x_res, _ = sb("x_res", [P, 2, D], F32, 2 * D * F)
        y_out, _ = sb("y_out", [P, 2, D], F32, 2 * D * F)
        ident, _ = sb("ident", [P, P], F32, P * F)
        ident2, _ = sb("ident2", [P, P], F32, P * F)
        row_sum, _ = sb("row_sum", [P, NB], F32, NB * F)
        col_part, _ = sb("col_part", [P, NB, NB], F32, NB * NB * F)
        col_sum, _ = sb("col_sum", [P, NB], F32, NB * F)
        deg, _ = sb("deg", [P, NB], F32, NB * F)
        deg_pos, _ = sb("deg_pos", [P, NB], F32, NB * F)
        deg_root, _ = sb("deg_root", [P, NB], F32, NB * F)
        deg_safe, _ = sb("deg_safe", [P, NB], F32, NB * F)
        root_inv, _ = sb("root_inv", [P, NB], F32, NB * F)
        dinv, _ = sb("dinv", [P, NB], F32, NB * F)
        dinv_half, _ = sb("dinv_half", [P, NB], F32, NB * F)
        eps, _ = sb("eps", [P, 1], F32, F)
        stats, _ = sb("stats", [P, 2, 6], F32, 12 * F)
        mean_var, _ = sb("mean_var", [P, 2, 2], F32, 4 * F)
        std, _ = sb("std", [P, 2], F32, 2 * F)
        rstd, _ = sb("rstd", [P, 2], F32, 2 * F)

        tp = ctx.enter_context(nc.psum_tensor("tp", [P, 2, NB, P], F32))
        acc = [tp[:, 1, 4 * j:4 * j + 4, :].rearrange("p a b -> p (a b)") for j in range(2)]

        s_ident = sem("ident_made")
        s_ident2 = sem("ident2_made")
        s_ring = [sem(f"ring_loaded{s}") for s in range(RING)]
        s_row = [sem(f"row_loaded{s}") for s in range(2)]
        s_col = [sem(f"col_loaded{s}") for s in range(2)]
        s_x = [sem(f"x_loaded{g}") for g in range(NB // XG)]
        s_stored = [sem(f"at_stored{s}") for s in range(2)]
        s_at = [sem(f"at_reloaded{s}") for s in range(2)]
        s_xres = [sem(f"xres_loaded{s}") for s in range(2)]
        s_out = [sem(f"out_stored{s}") for s in range(2)]
        s_rsum = sem("row_summed")
        s_csum = sem("col_summed")
        s_tr = sem("transposed")
        s_evac = sem("at_copied")
        s_diag = sem("diag_added")
        s_w = sem("w_summed")
        s_hi = sem("hi_ready")
        s_lo = sem("lo_ready")
        s_mm = sem("panel_done")
        s_deg = sem("deg_step")
        s_root = sem("deg_rooted")
        s_uh = sem("u_hi_ready")
        s_ul = sem("u_lo_ready")
        s_zh = sem("z_hi_ready")
        s_zl = sem("z_lo_ready")
        s_res = sem("residual_added")
        s_stat = sem("stats_made")
        s_var = sem("var_made")
        s_std = sem("std_made")
        s_rstd = sem("rstd_made")
        s_y = sem("y_normalised")

        block = ctx.enter_context(nc.Block())

        def chunk(t, slot, c):
            return t[:, slot, c * CB:(c + 1) * CB, :]

        @block.sync
        def _(sp):
            def load_ring(r, s):
                sp.dma_start(row_ring[:, s].rearrange("p b c -> p (b c)"), a_rows[r]).then_inc(s_ring[s], 16)

            sp.dma_start(rows[:, 0].rearrange("p b c -> p (b c)"), a_rows[0]).then_inc(s_row[0], 16)
            sp.dma_start(cols[:, 0], a_cols[0]).then_inc(s_col[0], 16)
            sp.dma_start(rows[:, 1].rearrange("p b c -> p (b c)"), a_rows[1]).then_inc(s_row[1], 16)
            sp.dma_start(cols[:, 1], a_cols[1]).then_inc(s_col[1], 16)
            for s in range(RING):
                load_ring(2 + s, s)
            with sp.Fori(1, (NB - 2) // RING) as i:
                for s in range(RING):
                    sp.wait_ge(s_tr, RING * i + s - RING + 3)
                    sp.wait_ge(s_rsum, RING * i + s - RING + 3)
                    load_ring(RING * i + s + 2, s)
            for r in range(2 + (NB - 2) // RING * RING, NB):
                sp.wait_ge(s_tr, r - RING + 1)
                sp.wait_ge(s_rsum, r - RING + 1)
                load_ring(r, (r - 2) % RING)
            for g in range(NB // XG):
                sp.dma_start(x_in[:, g * XG:(g + 1) * XG], x_blocks[:, g * XG:(g + 1) * XG]).then_inc(s_x[g], 16)

            def turn_over(m, i, j):
                sp.wait_ge(s_evac, HALF * m + HALF)
                sp.dma_start(at_scratch[m], rows[:, j]).then_inc(s_stored[j], 16)

            def load_next(m, i, j):
                sp.wait_ge(s_stored[j], 16 * i + 16)
                sp.wait_ge(s_w, HALF * m + HALF)
                sp.dma_start(rows[:, j].rearrange("p b c -> p (b c)"), a_rows[m + 2]).then_inc(s_row[j], 16)
                sp.wait_ge(s_lo, HALF * m + HALF)
                sp.dma_start(cols[:, j], a_cols[m + 2]).then_inc(s_col[j], 16)

            with sp.Fori(0, NB // 2 - 1) as i:
                for j in range(2):
                    turn_over(2 * i + j, i, j)
                    load_next(2 * i + j, i, j)
            for j in range(2):
                turn_over(NB - 2 + j, NB // 2 - 1, j)
            for j in range(2):
                sp.wait_ge(s_stored[j], 16 * (NB // 2))

            def load_at(q, j):
                sp.dma_start(cols[:, j], at_scratch[q]).then_inc(s_at[j], 16)
                sp.dma_start(x_res[:, j], x_rows[q]).then_inc(s_xres[j], 16)

            for j in range(2):
                sp.wait_ge(s_lo, HALF * (NB - 2 + j) + HALF)
                load_at(j, j)

            def store(q, j):
                sp.wait_ge(s_y, q + 1)
                sp.dma_start(out_rows[q], y_out[:, j]).then_inc(s_out[j], 16)

            with sp.Fori(0, NB // 2 - 1) as i:
                for j in range(2):
                    q = 2 * i + j
                    sp.wait_ge(s_lo, HALF * (NB + q) + HALF)
                    sp.dma_start(cols[:, j], at_scratch[q + 2]).then_inc(s_at[j], 16)
                    sp.wait_ge(s_res, q + 1)
                    sp.dma_start(x_res[:, j], x_rows[q + 2]).then_inc(s_xres[j], 16)
                    store(q, j)
            for q in range(NB - 2, NB):
                store(q, q % 2)
            for j in range(2):
                sp.wait_ge(s_out[j], 16 * (NB // 2))

        @block.gpsimd
        def _(pool):
            nc.gpsimd.memset(ident[:], 0.0).then_inc(s_ident, 1)
            nc.gpsimd.memset(ident2[:], 0.0).then_inc(s_ident2, 1)
            pool.wait_ge(s_ident, 1)
            nc.gpsimd.affine_select(out=ident[:], in_=ident[:], compare_op=ALU.not_equal, fill=1.0, base=0,
                                    pattern=[[-1, P]], channel_multiplier=1).then_inc(s_ident, 1)
            pool.wait_ge(s_ident2, 1)
            nc.gpsimd.affine_select(out=ident2[:], in_=ident2[:], compare_op=ALU.not_equal, fill=2.0, base=0,
                                    pattern=[[-1, P]], channel_multiplier=1).then_inc(s_ident2, 1)

        @block.tensor
        def _(pe):
            def transposes(src, half):
                for k in range(NB):
                    last = nc.tensor.transpose(tp[:, half, k, :], src[:, k, :], ident[:])
                last.then_inc(s_tr, 1)

            def products(slot, mov_hi, mov_lo, ready):
                for k in range(NB):
                    ready(k)
                    nc.tensor.matmul(acc[slot], w_hi[:, slot, k, :], mov_hi[:, k, :], start=(k == 0), stop=False)
                    nc.tensor.matmul(acc[slot], w_hi[:, slot, k, :], mov_lo[:, k, :], start=False, stop=False)
                    last = nc.tensor.matmul(acc[slot], w_lo[:, slot, k, :], mov_hi[:, k, :], start=False,
                                            stop=(k == NB - 1))
                last.then_inc(s_mm, 1)

            pe.wait_ge(s_ident, 2)
            for r in range(2):
                pe.wait_ge(s_row[r], 16)
                transposes(rows[:, r], r)

            def load_step(r, i, s):
                pe.wait_ge(s_ring[s], 16 * i + 16)
                pe.wait_ge(s_csum, r - 1)
                transposes(row_ring[:, s], s % 2)

            with pe.Fori(0, (NB - 2) // RING) as i:
                for s in range(RING):
                    load_step(RING * i + s + 2, i, s)
            for r in range(2 + (NB - 2) // RING * RING, NB):
                load_step(r, (r - 2) // RING, (r - 2) % RING)
            pe.wait_ge(s_csum, NB)

            def panel_ready(g, k):
                if k % CB == 0:
                    pe.wait_ge(s_lo, HALF * g + k // CB + 1)

            def first(k):
                panel_ready(0, k)
                pe.wait_ge(s_ul, k + 1)

            products(0, u_hi, u_lo, first)

            def step1(m, i, j):
                n_i, n_j = (i, 1) if j == 0 else (i + 1, 0)
                pe.wait_ge(s_row[n_j], 16 * n_i + 16)
                pe.wait_ge(s_evac, HALF * m + HALF)
                transposes(rows[:, n_j], 0)

            def mult1(m, j):
                pe.wait_ge(s_zl, m - 1)
                products(j, u_hi, u_lo, lambda k: panel_ready(m, k))

            step1(1, 0, 1)
            products(1, u_hi, u_lo, lambda k: panel_ready(1, k))
            with pe.Fori(1, NB // 2 - 1) as i:
                for j in range(2):
                    step1(2 * i + j, i, j)
                    mult1(2 * i + j, j)
            step1(NB - 2, NB // 2 - 1, 0)
            mult1(NB - 2, 0)
            mult1(NB - 1, 1)

            def first2(k):
                panel_ready(NB, k)
                if k == NB - 1:
                    pe.wait_ge(s_zl, NB)
            pe.wait_ge(s_zl, NB - 1)
            products(0, z_hi, z_lo, first2)
            products(1, z_hi, z_lo, lambda k: panel_ready(NB + 1, k))
            with pe.Fori(1, NB // 2) as i:
                for j in range(2):
                    pe.wait_ge(s_res, 2 * i + j - 1)
                    products(j, z_hi, z_lo, lambda k: panel_ready(NB + 2 * i + j, k))

        @block.scalar
        def _(act):
            def row_sum_of(src, r, j, again):
                if again:
                    act.wait_ge(s_rsum, r - 1)
                nc.scalar.activation(junk[:, j], src, ACT.Copy, accum_out=row_sum[:, bass.ds(r, 1)]).then_inc(s_rsum, 1)

            def copy_at(m, slot, half):
                act.wait_ge(s_tr, m)
                for c in range(HALF):
                    nc.scalar.activation(chunk(rows, slot, c), chunk(tp, half, c), ACT.Copy).then_inc(s_evac, 1)

            def split_hi(g, slot):
                for c in range(HALF):
                    nc.scalar.activation(chunk(w_hi, slot, c), chunk(cols, slot, c), ACT.Copy).then_inc(s_hi, 1)

            for r in range(2):
                act.wait_ge(s_row[r], 16)
                row_sum_of(rows[:, r], r, r, False)
                act.wait_ge(s_rsum, r + 1)
                copy_at(r + 1, r, r)
            for r in range(2):
                act.wait_ge(s_w, HALF * r + HALF)
                split_hi(r, r)
            with act.Fori(0, (NB - 2) // RING) as i:
                for s in range(RING):
                    act.wait_ge(s_ring[s], 16 * i + 16)
                    row_sum_of(row_ring[:, s], RING * i + s + 2, s % 2, True)
            for r in range(2 + (NB - 2) // RING * RING, NB):
                act.wait_ge(s_ring[(r - 2) % RING], 16 * ((r - 2) // RING) + 16)
                row_sum_of(row_ring[:, (r - 2) % RING], r, r % 2, True)
            act.wait_ge(s_deg, 4)
            nc.scalar.activation(deg_root[:], deg_safe[:], ACT.Sqrt).then_inc(s_root, 1)
            act.wait_ge(s_deg, 7)
            for k in range(NB):
                if k % XG == 0:
                    act.wait_ge(s_x[k // XG], 16)
                nc.scalar.activation(u_hi[:, k], x_in[:, k], ACT.Copy, scale=dinv[:, k:k + 1]).then_inc(s_uh, 1)

            def z_high(m, j):
                act.wait_ge(s_mm, m + 1)
                nc.scalar.activation(z_hi[:, m], acc[j], ACT.Copy, scale=dinv_half[:, bass.ds(m, 1)]).then_inc(s_zh, 1)

            def step1(m, j):
                copy_at(m + NB, 1 - j, 0)
                for c in range(HALF):
                    act.wait_ge(s_w, HALF * (m + 1) + c + 1)
                    if c == 0:
                        act.wait_ge(s_mm, m)
                    nc.scalar.activation(chunk(w_hi, 1 - j, c), chunk(cols, 1 - j, c), ACT.Copy).then_inc(s_hi, 1)
                z_high(m, j)

            z_high(0, 0)
            step1(1, 1)
            with act.Fori(1, NB // 2 - 1) as i:
                for j in range(2):
                    step1(2 * i + j, j)
            step1(NB - 2, 0)

            def high2(q, i, j):
                act.wait_ge(s_at[j], 16 * i + 16)
                act.wait_ge(s_mm, NB + q - 1)
                split_hi(NB + q, j)

            high2(0, 0, 0)
            z_high(NB - 1, 1)

            def root(q, j):
                act.wait_ge(s_var, q + 1)
                nc.scalar.activation(std[:, j:j + 1], mean_var[:, j, 1:2], ACT.Sqrt, bias=eps[:]).then_inc(s_std, 1)

            with act.Fori(0, NB // 2 - 1) as i:
                for j in range(2):
                    n_i, n_j = (i, 1) if j == 0 else (i + 1, 0)
                    high2(2 * i + j + 1, n_i, n_j)
                    root(2 * i + j, j)
            high2(NB - 1, NB // 2 - 1, 1)
            root(NB - 2, 0)
            root(NB - 1, 1)

        @block.vector
        def _(dve):
            nc.vector.memset(eps[:], EPS)

            def sum_w(m, i, j):
                dve.wait_ge(s_col[j], 16 * i + 16)
                nc.vector.tensor_tensor(cols[:, j, m], cols[:, j, m], ident2[:], ALU.add).then_inc(s_diag, 1)
                dve.wait_ge(s_diag, m + 1)
                for c in range(HALF):
                    dve.wait_ge(s_evac, HALF * m + c + 1)
                    nc.vector.tensor_tensor(chunk(cols, j, c), chunk(rows, j, c), chunk(cols, j, c),
                                            ALU.add).then_inc(s_w, 1)

            def split_lo(g, j):
                for c in range(HALF):
                    dve.wait_ge(s_hi, HALF * g + c + 1)
                    nc.vector.tensor_tensor(chunk(w_lo, j, c), chunk(cols, j, c), chunk(w_hi, j, c),
                                            ALU.subtract).then_inc(s_lo, 1)

            def col_sum_of(r, src):
                nc.vector.tensor_reduce(col_part[:, r, :], src, AX.X, ALU.add).then_inc(s_csum, 1)

            dve.wait_ge(s_ident2, 2)
            for r in range(2):
                dve.wait_ge(s_evac, HALF * r + HALF)
                col_sum_of(r, rows[:, r])
            for m in range(2):
                sum_w(m, 0, m)
            for m in range(2):
                split_lo(m, m)
            with dve.Fori(0, (NB - 2) // RING) as i:
                for s in range(RING):
                    dve.wait_ge(s_tr, RING * i + s + 3)
                    col_sum_of(RING * i + s + 2, tp[:, s % 2])
            for r in range(2 + (NB - 2) // RING * RING, NB):
                dve.wait_ge(s_tr, r + 1)
                col_sum_of(r, tp[:, r % 2])
            dve.wait_ge(s_csum, NB)
            nc.vector.tensor_reduce(col_sum[:], col_part[:].rearrange("p r k -> p k r"), AX.X,
                                    ALU.add).then_inc(s_deg, 1)
            dve.wait_ge(s_rsum, NB)
            dve.wait_ge(s_deg, 1)
            nc.vector.tensor_tensor(deg[:], row_sum[:], col_sum[:], ALU.add).then_inc(s_deg, 1)
            dve.wait_ge(s_deg, 2)
            nc.vector.tensor_scalar(deg[:], deg[:], 0.5, 1.0, ALU.mult, ALU.add).then_inc(s_deg, 1)
            dve.wait_ge(s_deg, 3)
            nc.vector.tensor_scalar(deg_safe[:], deg[:], TINY, None, ALU.max).then_inc(s_deg, 1)
            nc.vector.tensor_scalar(deg_pos[:], deg[:], 0.0, None, ALU.is_gt)
            dve.wait_ge(s_root, 1)
            nc.vector.reciprocal(root_inv[:], deg_root[:]).then_inc(s_deg, 1)
            dve.wait_ge(s_deg, 5)
            nc.vector.tensor_tensor(dinv[:], root_inv[:], deg_pos[:], ALU.mult).then_inc(s_deg, 1)
            dve.wait_ge(s_deg, 6)
            nc.vector.tensor_scalar(dinv_half[:], dinv[:], 0.5, None, ALU.mult).then_inc(s_deg, 1)
            for k in range(NB):
                dve.wait_ge(s_uh, k + 1)
                nc.vector.scalar_tensor_tensor(u_lo[:, k], x_in[:, k], dinv[:, k:k + 1], u_hi[:, k], ALU.mult,
                                               ALU.subtract).then_inc(s_ul, 1)

            def z_low(m, j):
                dve.wait_ge(s_zh, m + 1)
                nc.vector.scalar_tensor_tensor(z_lo[:, m], acc[j], dinv_half[:, bass.ds(m, 1)], z_hi[:, m], ALU.mult,
                                               ALU.subtract).then_inc(s_zl, 1)

            def step1(m, i, j):
                n_i, n_j = (i, 1) if j == 0 else (i + 1, 0)
                sum_w(m + 1, n_i, n_j)
                split_lo(m + 1, n_j)
                z_low(m, j)

            z_low(0, 0)
            step1(1, 0, 1)
            with dve.Fori(1, NB // 2 - 1) as i:
                for j in range(2):
                    step1(2 * i + j, i, j)
            step1(NB - 2, NB // 2 - 1, 0)
            split_lo(NB, 0)
            z_low(NB - 1, 1)

            def finish(q, i, j, stored):
                dve.wait_ge(s_xres[j], 16 * i + 16)
                dve.wait_ge(s_mm, NB + q + 1)
                if stored:
                    dve.wait_ge(s_out[j], 16 * i)
                nc.vector.tensor_tensor(y_out[:, j], acc[j], x_res[:, j], ALU.add).then_inc(s_res, 1)
                dve.wait_ge(s_res, q + 1)
                nc.vector.bn_stats(stats[:, j], y_out[:, j]).then_inc(s_stat, 1)
                dve.wait_ge(s_ident2, 2)
                dve.wait_ge(s_stat, q + 1)
                nc.vector.bn_aggr(mean_var[:, j], stats[:, j]).then_inc(s_var, 1)
                dve.wait_ge(s_std, q + 1)
                nc.vector.reciprocal(rstd[:, j:j + 1], std[:, j:j + 1]).then_inc(s_rstd, 1)
                dve.wait_ge(s_rstd, q + 1)
                nc.vector.tensor_scalar(y_out[:, j], y_out[:, j], mean_var[:, j, 0:1], rstd[:, j:j + 1],
                                        ALU.subtract, ALU.mult).then_inc(s_y, 1)

            for j in range(2):
                split_lo(NB + j + 1, 1 - j)
                finish(j, 0, j, False)
            with dve.Fori(1, NB // 2 - 1) as i:
                for j in range(2):
                    split_lo(NB + 2 * i + j + 1, 1 - j)
                    finish(2 * i + j, i, j, True)
            split_lo(2 * NB - 1, 1)
            finish(NB - 2, NB // 2 - 1, 0, True)
            finish(NB - 1, NB // 2 - 1, 1, True)


def kernel(x, adj):
    import numpy as np

    import concourse.bacc as bacc
    from concourse import mybir
    from concourse.bass_utils import run_bass_kernel_spmd

    nc = bacc.Bacc("TRN2", target_bir_lowering=False, num_devices=1)
    arrays = {"x": np.ascontiguousarray(x), "adj": np.ascontiguousarray(adj)}
    aps = [nc.dram_tensor(n, a.shape, mybir.dt.float32, kind="ExternalInput").ap() for n, a in arrays.items()]
    out = nc.dram_tensor("out", arrays["x"].shape, mybir.dt.float32, kind="ExternalOutput").ap()
    build(nc, *aps, out)
    return run_bass_kernel_spmd(nc, [arrays], core_ids=[0]).results[0]["out"]
```

```python
def build(nc, x, adj, out):
    from contextlib import ExitStack

    import concourse.bass as bass
    from concourse import mybir

    F32, F32R, BF16 = mybir.dt.float32, mybir.dt.float32r, mybir.dt.bfloat16
    ALU = mybir.AluOpType
    ACT = mybir.ActivationFunctionType
    AX = mybir.AxisListType

    P = 128
    N, D = x.shape
    NB = N // P
    G = 4
    NR = NB - G
    CB = 4
    NC = NB // CB
    DEPTH = 4
    LOTS = 8
    FIRST_M, CS_AFTER = 1, 1
    LEFT = [3, 3, 3, 3, 4, 4] + [5] * (NB - 6)
    STORE_FIRST_AFTER = 11
    FIRST_SUM, FIRST_HIGH, FIRST_LOW = {0: (0, 1), 1: (3,)}, {0: (0, 1), 1: (2, 3)}, {1: (1,), 2: (2, 3)}
    EPS = 1e-5
    TINY = 1e-30
    F = 4

    a_rows = adj.rearrange("(b p) n -> b p n", p=P)
    a_cols = adj.rearrange("(k p) (m c) -> m p k c", p=P, c=P)
    x_rows = x.rearrange("(b p) d -> b p d", p=P)
    out_rows = out.rearrange("(b p) d -> b p d", p=P)
    at_scratch = nc.dram_tensor("at_scratch", [NR, P, NB, P], F32).ap()

    ctx = ExitStack()
    with ctx:
        place = [16640]

        def at(name, shape, dt, offset):
            return nc.alloc_sbuf_tensor_at(name, shape, dt, offset=offset)

        def sb(name, shape, dt):
            size = F
            for n in shape[1:]:
                size *= n
            offset = place[0]
            place[0] += -(-size // 32) * 32
            return at(name, shape, dt, offset), offset

        def sem(name):
            return ctx.enter_context(nc.semaphore(name))

        u_hi, _ = sb("u_hi", [P, NB, D], F32R)
        u_lo, u_lo_at = sb("u_lo", [P, NB, D], F32R)
        x_in = at("x_in", [P, NB, D], F32, u_lo_at)
        z_hi, z_hi_at = sb("z_hi", [P, NB, D], F32R)
        z_lo, z_lo_at = sb("z_lo", [P, NB, D], F32R)
        w0_hi = at("w0_hi", [P, LOTS, G, P], F32R, z_hi_at)
        w0_lo = at("w0_lo", [P, LOTS, G, P], F32R, z_lo_at)
        rows_x = at("rows_x", [P, DEPTH - 2, NB, P], F32, z_hi_at + LOTS * G * P * F)
        cols_x = at("cols_x", [P, DEPTH - 2, NB, P], F32, z_lo_at + LOTS * G * P * F)
        w_hi, w_hi_at = sb("w_hi", [P, 2, NB, P], F32R)
        w_lo, w_lo_at = sb("w_lo", [P, 2, NB, P], F32R)
        at_first = at("at_first", [P, NB, P], F32, w_lo_at + NB * P * F)
        junk = at("junk", [P, 2, NB, P], BF16, w_hi_at + NB * P * F)
        rows, _ = sb("rows", [P, 2, NB, P], F32)
        cols, _ = sb("cols", [P, 2, NB, P], F32)
        col_acc, col_acc_at = sb("col_acc", [P, NB, P], F32)
        x_res = at("x_res", [P, 2, D], F32, col_acc_at)
        y_out = at("y_out", [P, 2, D], F32, col_acc_at + 2 * D * F)
        ident, _ = sb("ident", [P, P], F32)
        ident2, _ = sb("ident2", [P, P], F32)
        ones, _ = sb("ones", [P, 1], F32)
        mhalf, _ = sb("mhalf", [P, 1], F32)
        row_sum, _ = sb("row_sum", [P, 2, NB], F32)
        deg_part, _ = sb("deg_part", [P, NB], F32)
        deg, _ = sb("deg", [P, NB], F32)
        deg_pos, _ = sb("deg_pos", [P, NB], F32)
        deg_safe, _ = sb("deg_safe", [P, NB], F32)
        deg_pow, _ = sb("deg_pow", [P, NB], F32)
        dinv, _ = sb("dinv", [P, NB], F32)
        dinv_half, _ = sb("dinv_half", [P, NB], F32)
        stats, _ = sb("stats", [P, 2, 6], F32)
        mean_var, _ = sb("mean_var", [P, 2, 2], F32)
        var_eps, _ = sb("var_eps", [P, 2], F32)
        rstd, _ = sb("rstd", [P, 2], F32)

        ps = ctx.enter_context(nc.psum_tensor("ps", [P, 8, CB * P], F32))
        acc0 = [ps[:, m] for m in range(G)]
        tp = [ps[:, n].rearrange("p (b c) -> p b c", c=P) for n in (G, G + 1)]
        csum = ps[:, G + 2]
        acc = [ps[:, G + 3], ps[:, G + 2]]

        s_const = sem("constants_made")
        s_ident = sem("ident_made")
        s_rx = [sem(f"row_and_x_loaded{s}") for s in range(4)]
        s_c = [sem(f"col_part_loaded{s}") for s in range(4)]
        s_r0 = [sem(f"row0_half_loaded{h}") for h in range(2)]
        s_c0 = [sem(f"col0_half_loaded{h}") for h in range(2)]
        s_x0 = sem("x0_loaded")
        s_t0 = sem("g0_transposed")
        s_diag0 = sem("g0_diag_added")
        s_add0 = sem("g0_chunk_added")
        s_hi0 = sem("g0_hi_ready")
        s_lo0 = sem("g0_lo_ready")
        s_hiw = sem("g0_mirror_hi_ready")
        s_rsum = sem("row_summed")
        s_cnext = sem("col_acc_next_made")
        s_cmid = sem("col_acc_near_made")
        s_cacc = sem("col_acc_made")
        s_ones = sem("col_sum_in_psum")
        s_dpart = sem("deg_part_made")
        s_deg = sem("deg_made")
        s_safe = sem("deg_safe_made")
        s_pos = sem("deg_pos_made")
        s_pow = sem("deg_pow_made")
        s_dinv = sem("dinv_made")
        s_dhalf = sem("dinv_half_made")
        s_uh = sem("u_hi_ready")
        s_ul = sem("u_lo_ready")
        s_prod = sem("g0_step_done")
        s_row = [sem(f"row_loaded{s}") for s in range(2)]
        s_col = [sem(f"col_loaded{s}") for s in range(2)]
        s_stored = [sem(f"at_stored{s}") for s in range(2)]
        s_row2 = [sem(f"row_loaded_again{s}") for s in range(2)]
        s_at = [sem(f"at_reloaded{s}") for s in range(2)]
        s_xres = [sem(f"xres_loaded{s}") for s in range(2)]
        s_out = [sem(f"out_stored{s}") for s in range(2)]
        s_tr = sem("transposed")
        s_evac = sem("at_copied")
        s_diag = sem("diag_added")
        s_w = sem("w_summed")
        s_hi = sem("hi_ready")
        s_lo = sem("lo_ready")
        s_mm = sem("panel_done")
        s_zh = sem("z_hi_ready")
        s_zl = sem("z_lo_ready")
        s_res = sem("residual_added")
        s_stat = sem("stats_made")
        s_var = sem("var_made")
        s_veps = sem("var_eps_made")
        s_rstd = sem("rstd_made")
        s_y = sem("y_normalised")

        block = ctx.enter_context(nc.Block())

        def piece(t, k, b0, b1):
            slot, shift = k % DEPTH, 0
            if k >= NB - DEPTH:
                slot, shift = 2 + k % 2, k - DEPTH * ((k - NB + DEPTH) // 2)
            of = ((rows, cols), (rows_x, cols_x))[slot // 2][t]
            return of[:, slot % 2, b0 - shift:b1 - shift, :]

        def chunks_of(k):
            return [(b, min(b + CB, NB)) for b in range(k, NB, CB)]

        def mirrored(k):
            return NR <= k < NB - 1

        def chunk_at(k):
            return sum(len(chunks_of(j)) + mirrored(j) for j in range(k))

        def chunk_end(k):
            return chunk_at(k) + len(chunks_of(k))

        def row_x_count(k):
            return 32 * (k // 4 + (k % 4 > 0))

        def col_count(k):
            return 16 * (k // 4 + (k % 4 > 0))

        def pieces_of(k):
            cs = chunks_of(k)
            if len(cs) == 1:
                return [(k, NB, chunk_end(k))]
            first = (len(cs) + 1) // 2
            return [(k, cs[first - 1][1], chunk_at(k) + first), (cs[first][0], NB, chunk_end(k))]

        def pieces_end(k):
            return sum(len(pieces_of(j)) for j in range(k + 1))

        HALF = NB // 2

        @block.sync
        def _(sp):
            def load_first():
                for h in range(2):
                    sp.dma_start(rows[:, 0, HALF * h:HALF * h + HALF].rearrange("p b c -> p (b c)"),
                                 a_rows[0, :, HALF * h * P:(HALF * h + HALF) * P]).then_inc(s_r0[h], 16)
                for h in range(2):
                    b = max(1, HALF * h)
                    sp.dma_start(piece(1, 0, b, HALF * h + HALF), a_cols[0, :, b:HALF * h + HALF]).then_inc(s_c0[h], 16)
                sp.dma_start(x_in[:, 0], x_rows[0]).then_inc(s_x0, 16)

            def load_step(k):
                if k >= DEPTH:
                    sp.wait_ge(s_t0, chunk_end(k - DEPTH))
                if DEPTH <= k < NB - DEPTH:
                    sp.wait_ge(s_rsum, pieces_end(k - DEPTH))
                    sp.wait_ge(s_cacc, k - DEPTH + 1)
                    sp.wait_ge(s_lo0, k - DEPTH + 1)
                sp.dma_start(piece(0, k, k, NB).rearrange("p b c -> p (b c)"),
                             a_rows[k, :, k * P:N]).then_inc(s_rx[k % 4], 16)
                if k == DEPTH:
                    sp.wait_ge(s_lo, NC)
                if k < NB - 1:
                    sp.dma_start(piece(1, k, k + 1, NB), a_cols[k, :, k + 1:NB]).then_inc(s_c[k % 4], 16)
                sp.dma_start(x_in[:, k], x_rows[k]).then_inc(s_rx[k % 4], 16)

            load_first()
            for k in range(1, NB):
                load_step(k)
                if k == STORE_FIRST_AFTER:
                    sp.wait_ge(s_evac, NC)
                    sp.dma_start(at_scratch[0], at_first[:]).then_inc(s_stored[0], 16)
            for j in (1, 0):
                k = NB - 2 * DEPTH + j
                sp.wait_ge(s_t0, chunk_end(k))
                sp.wait_ge(s_rsum, pieces_end(k))
                sp.wait_ge(s_cacc, k + 1)
                sp.wait_ge(s_lo0, k + 1)
                sp.dma_start(rows[:, j].rearrange("p b c -> p (b c)"), a_rows[2 - j]).then_inc(s_row[j], 16)
                sp.dma_start(cols[:, j], a_cols[2 - j]).then_inc(s_col[j], 16)

            def store_at(p, j):
                sp.wait_ge(s_evac, NC * p + NC)
                sp.dma_start(at_scratch[p], rows[:, j]).then_inc(s_stored[j], 16)

            def row_slot_free(p, i, j):
                sp.wait_ge(s_stored[j], 16 * i + 16)
                sp.wait_ge(s_w, NC * p + NC)

            def turn(p, i, j):
                store_at(p, j)
                row_slot_free(p, i, j)
                sp.dma_start(rows[:, j].rearrange("p b c -> p (b c)"), a_rows[p + 2]).then_inc(s_row[j], 16)
                sp.wait_ge(s_lo, NC * p + NC)
                sp.dma_start(cols[:, j], a_cols[p + 2]).then_inc(s_col[j], 16)

            turn(1, 0, 1)
            with sp.Fori(1, NR // 2 - 1) as i:
                for j in range(2):
                    turn(2 * i + j, i, j)
            for j in range(2):
                p = NR - 2 + j
                store_at(p, j)
                row_slot_free(p, NR // 2 - 1, j)
                sp.dma_start(rows[:, j].rearrange("p b c -> p (b c)"), a_rows[NR + j]).then_inc(s_row2[j], 16)
                sp.dma_start(x_res[:, j], x_rows[NR + j]).then_inc(s_xres[j], 16)
            for j in range(2):
                sp.wait_ge(s_lo, NC * (NR - 2 + j) + NC)
                sp.dma_start(cols[:, j], at_scratch[j]).then_inc(s_at[j], 16)

            def load_x(s, q, j):
                sp.wait_ge(s_res, s - 1)
                sp.dma_start(x_res[:, j], x_rows[q]).then_inc(s_xres[j], 16)

            def store(s, q, j):
                sp.wait_ge(s_y, s + 1)
                sp.dma_start(out_rows[q], y_out[:, j]).then_inc(s_out[j], 16)

            for s in range(2, G):
                sp.wait_ge(s_tr, NC * (NR + s - 1))
                sp.dma_start(rows[:, s % 2].rearrange("p b c -> p (b c)"), a_rows[NR + s]).then_inc(s_row2[s % 2], 16)
                load_x(s, NR + s, s % 2)
                store(s - 2, NR + s - 2, s % 2)
            for j in range(2):
                load_x(G + j, j, j)
                store(G - 2 + j, NB - 2 + j, j)
                sp.wait_ge(s_lo, NC * (NR + G + j) + NC)
                sp.dma_start(cols[:, j], at_scratch[2 + j]).then_inc(s_at[j], 16)
            with sp.Fori(1, NR // 2 - 1) as i:
                for j in range(2):
                    q = 2 * i + j
                    load_x(G + q, q, j)
                    store(G + q - 2, q - 2, j)
                    sp.wait_ge(s_lo, NC * (NB + q) + NC)
                    sp.dma_start(cols[:, j], at_scratch[q + 2]).then_inc(s_at[j], 16)
            for j in range(2):
                load_x(NB - 2 + j, NR - 2 + j, j)
                store(NB - 4 + j, NR - 4 + j, j)
            for j in range(2):
                store(NB - 2 + j, NR - 2 + j, j)
            for j in range(2):
                sp.wait_ge(s_out[j], 16 * (NB // 2))

        @block.gpsimd
        def _(pool):
            nc.gpsimd.memset(ones[:], 1.0).then_inc(s_const, 1)
            nc.gpsimd.memset(ident[:], 0.0).then_inc(s_const, 1)
            nc.gpsimd.memset(ident2[:], 0.0).then_inc(s_const, 1)
            nc.gpsimd.memset(mhalf[:], -0.5).then_inc(s_const, 1)
            nc.gpsimd.memset(col_acc[:], 0.0).then_inc(s_const, 1)
            pool.wait_ge(s_const, 5)
            for t, v in ((ident, 1.0), (ident2, 2.0)):
                nc.gpsimd.affine_select(out=t[:], in_=t[:], compare_op=ALU.not_equal, fill=v, base=0,
                                        pattern=[[-1, P]], channel_multiplier=1).then_inc(s_ident, 1)

            def invert_root(k):
                pool.wait_ge(s_safe, k + 1)
                nc.gpsimd.tensor_tensor(deg_pow[:, k:k + 1], deg_safe[:, k:k + 1], mhalf[:],
                                        ALU.pow).then_inc(s_pow, 1)
                pool.wait_ge(s_pow, k + 1)
                pool.wait_ge(s_pos, k + 1)
                nc.gpsimd.tensor_tensor(dinv[:, k:k + 1], deg_pow[:, k:k + 1], deg_pos[:, k:k + 1],
                                        ALU.mult).then_inc(s_dinv, 1)

            def accumulate(k, b0, b1, chunks, signal):
                pool.wait_ge(s_add0, chunks)
                return nc.gpsimd.tensor_tensor(col_acc[:, b0:b1], col_acc[:, b0:b1], piece(0, k, b0, b1),
                                               ALU.add).then_inc(signal, 1)

            for k in range(NB):
                n = chunk_at(k)
                b = k + 2
                if k < NB - 1:
                    if k >= 1:
                        pool.wait_ge(s_cacc, k)
                    accumulate(k, k + 1, b, n + 1, s_cnext)
                if len(chunks_of(k)) > 2:
                    b = k + 2 * CB
                    accumulate(k, k + 2, b, n + 2, s_cmid)
                invert_root(k)
                if b < NB:
                    accumulate(k, b, NB, chunk_end(k), s_cacc)

            def rstd_of(q, j):
                pool.wait_ge(s_veps, q + 1)
                nc.gpsimd.tensor_tensor(rstd[:, j:j + 1], var_eps[:, j:j + 1], mhalf[:], ALU.pow).then_inc(s_rstd, 1)

            with pool.Fori(0, NB // 2) as i:
                for j in range(2):
                    rstd_of(2 * i + j, j)

        @block.tensor
        def _(pe):
            def passes(out_, hi, lo, mov_hi, mov_lo, first, last):
                nc.tensor.matmul(out_, hi, mov_hi, start=first, stop=False)
                nc.tensor.matmul(out_, hi, mov_lo, start=False, stop=False)
                return nc.tensor.matmul(out_, lo, mov_hi, start=False, stop=last)

            def transposes(bank, src, s):
                for b in range(src.shape[1]):
                    last = nc.tensor.transpose(tp[bank][:, b], src[:, b], ident[:])
                last.then_inc(s, 1)

            def transpose_chunk(k, n, b0, b1):
                if n < 2:
                    pe.wait_ge(s_evac, n + NC - 1)
                else:
                    pe.wait_ge(s_add0, n - 1)
                if k == 0:
                    pe.wait_ge(s_c0[(b1 - 1) // HALF], 16)
                elif b0 == k:
                    pe.wait_ge(s_rx[k % 4], row_x_count(k))
                    if k < NB - 1:
                        pe.wait_ge(s_c[k % 4], col_count(k))
                for b in range(b0, b1):
                    src = piece(0 if b == k else 1, k, b, b + 1)[:, 0]
                    last = nc.tensor.transpose(tp[n % 2][:, b - b0], src, ident[:])
                last.then_inc(s_t0, 1)

            def mirror_step(k):
                n = chunk_end(k)
                pe.wait_ge(s_add0, n)
                transposes(n % 2, piece(0, k, k + 1, NB), s_t0)

            def col_sums(k):
                pe.wait_ge(s_cnext, k)
                pe.wait_ge(s_deg, k)
                nc.tensor.matmul(csum[:, k:k + 1], col_acc[:, k], ones[:], start=True, stop=True).then_inc(s_ones, 1)

            def multiply0(k, m):
                if m == 0:
                    pe.wait_ge(s_ul, k + 1)
                    pe.wait_ge(s_lo0, k + 1)
                    if k > NR:
                        pe.wait_ge(s_add0, chunk_end(k - 1) + 1)
                if m < G:
                    last = passes(acc0[m], w0_hi[:, k % LOTS, m], w0_lo[:, k % LOTS, m], u_hi[:, k], u_lo[:, k],
                                  k == 0, k == NB - 1)
                    if m == G - 1:
                        last.then_inc(s_prod, 1)
                else:
                    pe.wait_ge(s_lo, k // CB + 1)
                    last = passes(acc[0], w_hi[:, 0, k], w_lo[:, 0, k], u_hi[:, k], u_lo[:, k],
                                  k == 0, k == NB - 1)
                    if k == NB - 1:
                        last.then_inc(s_mm, 1)

            def chunk1(p, i, j, c):
                if c == 0:
                    pe.wait_ge(s_row[j], 16 * i + 16)
                n = NC * p + c
                if isinstance(n, int) and n < NC + 2:
                    pe.wait_ge(s_add0, chunk_end(NB - 1))
                else:
                    pe.wait_ge(s_evac, n - 1)
                transposes(c % 2, rows[:, j, CB * c:CB * c + CB], s_tr)

            pe.wait_ge(s_ident, 2)
            for c in range(NC):
                pe.wait_ge(s_r0[CB * c // HALF], 16)
                if c >= 2:
                    pe.wait_ge(s_evac, c - 1)
                transposes(c % 2, rows[:, 0, CB * c:CB * c + CB], s_tr)
            left_over = []
            for k in range(NB):
                if k >= 1 and mirrored(k - 1):
                    mirror_step(k - 1)
                for n, (b0, b1) in enumerate(chunks_of(k)):
                    if n >= FIRST_M and left_over:
                        multiply0(*left_over.pop(0))
                    transpose_chunk(k, chunk_at(k) + n, b0, b1)
                    if k >= 1 and n == min(CS_AFTER, len(chunks_of(k)) - 1):
                        col_sums(k)
                if k >= 1:
                    left_over += [(k - 1, m) for m in range(G + 1)]
                while len(left_over) > LEFT[k]:
                    multiply0(*left_over.pop(0))
            chunk1(1, 0, 1, 0)
            chunk1(1, 0, 1, 1)
            for k, m in left_over:
                multiply0(k, m)
            chunk1(1, 0, 1, 2)
            multiply0(NB - 1, 0)
            chunk1(1, 0, 1, 3)
            for m in range(1, G + 1):
                multiply0(NB - 1, m)

            def multiply(g, j, mov_hi, mov_lo, between, order=range(NB)):
                seen = set()
                for n, k in enumerate(order):
                    if k // CB not in seen:
                        seen.add(k // CB)
                        pe.wait_ge(s_lo, NC * g + k // CB + 1)
                    between(n)
                    last = passes(acc[j], w_hi[:, j, k], w_lo[:, j, k], mov_hi[:, k], mov_lo[:, k],
                                  n == 0, n == NB - 1)
                last.then_inc(s_mm, 1)

            AHEAD = {1: 0, 4: 1, 7: 2, 10: 3}

            def ahead1(p, i, j):
                return lambda k: chunk1(p, i, j, AHEAD[k]) if k in AHEAD else None

            multiply(1, 1, u_hi, u_lo, ahead1(2, 0, 0))
            with pe.Fori(0, NR // 2 - 2) as i:
                for j in range(2):
                    p = 2 * i + 2 + j
                    pe.wait_ge(s_zl, G + p - 1)
                    multiply(p, j, u_hi, u_lo, ahead1(p + 1, i + 1, 1 - j))
            pe.wait_ge(s_zl, G + NR - 3)
            multiply(NR - 2, 0, u_hi, u_lo, ahead1(NR - 1, NR // 2 - 1, 1))

            def chunk2(q, c):
                if c == 0:
                    pe.wait_ge(s_row2[q % 2], 16 * (q // 2) + 16)
                if NC * q + c < 2:
                    pe.wait_ge(s_evac, NC * NR)
                else:
                    pe.wait_ge(s_lo, NC * (NR + q) + c - 1)
                transposes(c % 2, rows[:, q % 2, CB * c:CB * c + CB], s_tr)

            def ahead2(q):
                return lambda k: chunk2(q, AHEAD[k]) if k in AHEAD and q < G else None

            pe.wait_ge(s_zl, G + NR - 2)
            multiply(NR - 1, 1, u_hi, u_lo, ahead2(0))

            def z_last(n):
                if n == NB - 1:
                    pe.wait_ge(s_zl, NB)
                ahead2(1)(n)

            pe.wait_ge(s_zl, NB - 1)
            multiply(NR, 0, z_hi, z_lo, z_last, [k for k in range(NB) if k != NR - 1] + [NR - 1])
            for s in range(1, G):
                if s >= 2:
                    pe.wait_ge(s_res, s - 1)
                multiply(NR + s, s % 2, z_hi, z_lo, ahead2(s + 1))
            with pe.Fori(0, NR // 2) as i:
                for j in range(2):
                    s = G + 2 * i + j
                    pe.wait_ge(s_res, s - 1)
                    multiply(NR + s, j, z_hi, z_lo, lambda n: None)

        @block.scalar
        def _(act):
            for c in range(NC):
                act.wait_ge(s_tr, c + 1)
                nc.scalar.activation(at_first[:, CB * c:CB * c + CB], tp[c % 2], ACT.Copy).then_inc(s_evac, 1)

            def high_first(c):
                act.wait_ge(s_w, c + 1)
                nc.scalar.activation(w_hi[:, 0, CB * c:CB * c + CB], cols[:, 0, CB * c:CB * c + CB],
                                     ACT.Copy).then_inc(s_hi, 1)

            for k in range(NB):
                if k >= 1 and mirrored(k - 1):
                    j = k - 1
                    act.wait_ge(s_t0, chunk_end(j) + 1)
                    act.wait_ge(s_prod, NB - LOTS)
                    nc.scalar.activation(w0_hi[:, k % LOTS:LOTS, j - NR], tp[chunk_end(j) % 2][:, 0:NB - k],
                                         ACT.Copy).then_inc(s_hiw, 1)
                if k >= 2:
                    act.wait_ge(s_rsum, pieces_end(k - 2))
                for t, (b0, b1, chunks) in enumerate(pieces_of(k)):
                    if k < NR:
                        act.wait_ge(s_add0, chunks)
                    else:
                        act.wait_ge(s_diag0, k - NR + 1)
                    nc.scalar.activation(junk[:, k % 2, b0:b1], piece(0, k, b0, b1), ACT.Copy,
                                         accum_out=row_sum[:, t, k:k + 1]).then_inc(s_rsum, 1)
                if k >= LOTS:
                    act.wait_ge(s_prod, k - LOTS + 1)
                b = max(k, NR)
                nc.scalar.activation(w0_hi[:, k % LOTS, b - NR:G], piece(0, k, b, NB), ACT.Copy).then_inc(s_hi0, 1)
                if k == 0:
                    act.wait_ge(s_x0, 16)
                act.wait_ge(s_dinv, k + 1)
                nc.scalar.activation(u_hi[:, k], x_in[:, k], ACT.Copy, scale=dinv[:, k:k + 1]).then_inc(s_uh, 1)
                for c in FIRST_HIGH.get(k, ()):
                    high_first(c)

            def copy_at(p, j, c):
                act.wait_ge(s_tr, NC * p + c + 1)
                nc.scalar.activation(rows[:, j, CB * c:CB * c + CB], tp[c % 2], ACT.Copy).then_inc(s_evac, 1)

            def high1(p, j, c):
                act.wait_ge(s_w, NC * p + c + 1)
                nc.scalar.activation(w_hi[:, j, CB * c:CB * c + CB], cols[:, j, CB * c:CB * c + CB],
                                     ACT.Copy).then_inc(s_hi, 1)

            def z_high(m, src):
                nc.scalar.activation(z_hi[:, m], src, ACT.Copy, scale=dinv_half[:, bass.ds(m, 1)]).then_inc(s_zh, 1)

            def panel1(p, j, mm):
                copy_at(p, j, 0)
                copy_at(p, j, 1)
                if mm is not None:
                    act.wait_ge(s_mm, mm)
                high1(p, j, 0)
                copy_at(p, j, 2)
                high1(p, j, 1)
                copy_at(p, j, 3)
                high1(p, j, 2)
                high1(p, j, 3)

            panel1(1, 1, None)
            act.wait_ge(s_prod, NB)
            act.wait_ge(s_dhalf, 1)
            for m in range(G):
                z_high(NR + m, acc0[m])
            act.wait_ge(s_mm, 1)
            z_high(0, acc[0])

            def step1(p, j):
                panel1(p + 1, 1 - j, p)
                act.wait_ge(s_mm, p + 1)
                z_high(p, acc[j])

            with act.Fori(0, NR // 2 - 1) as i:
                for j in (1, 0):
                    step1(2 * i + 2 - j, j)

            def high2(q, c):
                act.wait_ge(s_tr, NC * (NR + q) + c + 1)
                nc.scalar.activation(w_hi[:, q % 2, CB * c:CB * c + CB], tp[c % 2], ACT.Copy).then_inc(s_hi, 1)

            def high3(q, i, j):
                act.wait_ge(s_at[j], 16 * i + 16)
                act.wait_ge(s_mm, NR + q - 1)
                for c in range(NC):
                    nc.scalar.activation(w_hi[:, j, CB * c:CB * c + CB], cols[:, j, CB * c:CB * c + CB],
                                         ACT.Copy).then_inc(s_hi, 1)

            for q in range(G):
                act.wait_ge(s_mm, NR + q - 1)
                for c in range(NC):
                    high2(q, c)
                if q == 0:
                    act.wait_ge(s_mm, NR)
                    z_high(NR - 1, acc[1])
            with act.Fori(0, (NB - G) // 2) as i:
                for j in range(2):
                    high3(G + 2 * i + j, i, j)

        @block.vector
        def _(dve):
            dve.wait_ge(s_ident, 2)

            def add(out_, a, b, s):
                return nc.vector.tensor_tensor(out_, a, b, ALU.add).then_inc(s, 1)

            def degrees(k):
                two = len(pieces_of(k)) == 2
                made, signal = (deg_part, s_dpart) if two else (deg, s_deg)
                dve.wait_ge(s_rsum, pieces_end(k) - two)
                if k == 0:
                    nc.vector.tensor_scalar(made[:, 0:1], row_sum[:, 0, 0:1], 0.5, None, ALU.mult).then_inc(signal, 1)
                else:
                    dve.wait_ge(s_ones, k)
                    nc.vector.tensor_scalar(made[:, k:k + 1], csum[:, k:k + 1], row_sum[:, 0, k:k + 1], 0.5, ALU.add,
                                            ALU.mult).then_inc(signal, 1)
                if two:
                    dve.wait_ge(s_rsum, pieces_end(k))
                    dve.wait_ge(s_dpart, k + 1)
                    nc.vector.tensor_scalar(deg[:, k:k + 1], row_sum[:, 1, k:k + 1], 0.5, deg_part[:, k:k + 1],
                                            ALU.mult, ALU.add).then_inc(s_deg, 1)
                dve.wait_ge(s_deg, k + 1)
                one = 1.0 if k < NR else 0.0
                nc.vector.tensor_scalar(deg_safe[:, k:k + 1], deg[:, k:k + 1], one, TINY, ALU.add,
                                        ALU.max).then_inc(s_safe, 1)
                nc.vector.tensor_scalar(deg_pos[:, k:k + 1], deg[:, k:k + 1], -one, None, ALU.is_gt).then_inc(s_pos, 1)

            def u_low(k):
                dve.wait_ge(s_uh, k + 1)
                nc.vector.scalar_tensor_tensor(u_lo[:, k], x_in[:, k], dinv[:, k:k + 1], u_hi[:, k], ALU.mult,
                                               ALU.subtract).then_inc(s_ul, 1)

            def low(g, j, c, src):
                dve.wait_ge(s_hi, NC * g + c + 1)
                nc.vector.tensor_tensor(w_lo[:, j, CB * c:CB * c + CB], src, w_hi[:, j, CB * c:CB * c + CB],
                                        ALU.subtract).then_inc(s_lo, 1)

            def sum_first(c):
                b = CB * c
                if c == 0:
                    dve.wait_ge(s_add0, 1)
                    add(cols[:, 0, 0], rows[:, 0, 0], ident2[:], s_diag)
                    b = 1
                dve.wait_ge(s_evac, c + 1)
                add(cols[:, 0, b:CB * c + CB], at_first[:, b:CB * c + CB], cols[:, 0, b:CB * c + CB], s_w)

            for k in range(NB):
                if k >= 1 and mirrored(k - 1):
                    dve.wait_ge(s_hiw, k - NR)
                    nc.vector.tensor_tensor(w0_lo[:, k % LOTS:LOTS, k - 1 - NR], tp[chunk_end(k - 1) % 2][:, 0:NB - k],
                                            w0_hi[:, k % LOTS:LOTS, k - 1 - NR], ALU.subtract).then_inc(s_add0, 1)
                if k == 1:
                    dve.wait_ge(s_x0, 16)
                    u_low(0)
                    low(0, 0, 0, cols[:, 0, 0:CB])
                if k >= 1:
                    dve.wait_ge(s_rx[k % 4], row_x_count(k))
                n = chunk_at(k)
                for t, (b0, b1) in enumerate(chunks_of(k)):
                    dve.wait_ge(s_t0, n + 1)
                    w = piece(0, k, b0, b1)
                    add(w, tp[n % 2][:, 0:b1 - b0], w, s_add0)
                    n += 1
                    if k >= 2 and t == min(1, len(chunks_of(k)) - 1):
                        u_low(k - 1)
                if k >= NR:
                    diag = piece(0, k, k, k + 1)[:, 0]
                    dve.wait_ge(s_add0, n)
                    add(diag, diag, ident2[:], s_diag0)
                for c in FIRST_LOW.get(k, ()):
                    low(0, 0, c, cols[:, 0, CB * c:CB * c + CB])
                for c in FIRST_SUM.get(k, ()):
                    sum_first(c)
                degrees(k)
                if k == 0:
                    sum_first(2)
                b = max(k, NR)
                dve.wait_ge(s_hi0, k + 1)
                nc.vector.tensor_tensor(w0_lo[:, k % LOTS, b - NR:G], piece(0, k, b, NB),
                                        w0_hi[:, k % LOTS, b - NR:G], ALU.subtract).then_inc(s_lo0, 1)
            u_low(NB - 1)
            dve.wait_ge(s_dinv, NB)
            nc.vector.tensor_scalar(dinv_half[:], dinv[:], 0.5, None, ALU.mult).then_inc(s_dhalf, 1)

            def panel1(p, i, j):
                def sum_chunk(c):
                    dve.wait_ge(s_evac, NC * p + c + 1)
                    add(cols[:, j, CB * c:CB * c + CB], rows[:, j, CB * c:CB * c + CB],
                        cols[:, j, CB * c:CB * c + CB], s_w)

                dve.wait_ge(s_col[j], 16 * i + 16)
                add(cols[:, j, p], cols[:, j, p], ident2[:], s_diag)
                dve.wait_ge(s_diag, p + 1)
                sum_chunk(0)
                for c in range(1, NC):
                    sum_chunk(c)
                    low(p, j, c - 1, cols[:, j, CB * (c - 1):CB * c])
                low(p, j, NC - 1, cols[:, j, CB * (NC - 1):NB])

            def z_low(n, m, src):
                dve.wait_ge(s_zh, n + 1)
                nc.vector.scalar_tensor_tensor(z_lo[:, m], src, dinv_half[:, bass.ds(m, 1)], z_hi[:, m], ALU.mult,
                                               ALU.subtract).then_inc(s_zl, 1)

            dve.wait_ge(s_stored[0], 16)
            panel1(1, 0, 1)
            for m in range(G):
                z_low(m, NR + m, acc0[m])
            z_low(G, 0, acc[0])
            with dve.Fori(0, NR // 2 - 1) as i:
                for j in (1, 0):
                    p = 2 * i + 2 - j
                    panel1(p + 1, i + (1 - j), 1 - j)
                    z_low(G + p, p, acc[j])

            def low2(q):
                for c in range(NC):
                    low(NR + q, q % 2, c, tp[c % 2])

            def low3(q, j):
                for c in range(NC):
                    low(NR + q, j, c, cols[:, j, CB * c:CB * c + CB])

            def finish(q, i, j, again):
                dve.wait_ge(s_xres[j], 16 * i + 16)
                if again:
                    dve.wait_ge(s_out[j], 16 * i)
                dve.wait_ge(s_mm, NR + q + 1)
                add(y_out[:, j], acc[j], x_res[:, j], s_res)
                dve.wait_ge(s_res, q + 1)
                nc.vector.bn_stats(stats[:, j], y_out[:, j]).then_inc(s_stat, 1)
                dve.wait_ge(s_ident, 2)
                dve.wait_ge(s_stat, q + 1)
                nc.vector.bn_aggr(mean_var[:, j], stats[:, j]).then_inc(s_var, 1)
                dve.wait_ge(s_var, q + 1)
                nc.vector.tensor_scalar(var_eps[:, j:j + 1], mean_var[:, j, 1:2], EPS, None, ALU.add).then_inc(s_veps, 1)
                dve.wait_ge(s_rstd, q + 1)
                nc.vector.tensor_scalar(y_out[:, j], y_out[:, j], mean_var[:, j, 0:1], rstd[:, j:j + 1],
                                        ALU.subtract, ALU.mult).then_inc(s_y, 1)

            low2(0)
            z_low(NB - 1, NR - 1, acc[1])
            for q in range(G):
                if q < G - 1:
                    low2(q + 1)
                else:
                    low3(q + 1, 0)
                finish(q, q // 2, q % 2, q >= 2)
            with dve.Fori(0, (NB - G) // 2 - 1) as i:
                for j in range(2):
                    q = G + 2 * i + j
                    low3(q + 1, 1 - j)
                    finish(q, G // 2 + i, j, True)
            low3(NB - 1, 1)
            finish(NB - 2, NB // 2 - 1, 0, True)
            finish(NB - 1, NB // 2 - 1, 1, True)


def kernel(x, adj):
    import numpy as np

    import concourse.bacc as bacc
    from concourse import mybir
    from concourse.bass_utils import run_bass_kernel_spmd

    nc = bacc.Bacc("TRN2", target_bir_lowering=False, num_devices=1)
    arrays = {"x": np.ascontiguousarray(x), "adj": np.ascontiguousarray(adj)}
    aps = [nc.dram_tensor(n, a.shape, mybir.dt.float32, kind="ExternalInput").ap() for n, a in arrays.items()]
    out = nc.dram_tensor("out", arrays["x"].shape, mybir.dt.float32, kind="ExternalOutput").ap()
    build(nc, *aps, out)
    return run_bass_kernel_spmd(nc, [arrays], core_ids=[0]).results[0]["out"]
```

```python
def build(nc, x, adj, out):
    from contextlib import ExitStack

    import concourse.bass as bass
    from concourse import mybir

    F32, F32R, BF16 = mybir.dt.float32, mybir.dt.float32r, mybir.dt.bfloat16
    ALU = mybir.AluOpType
    ACT = mybir.ActivationFunctionType

    P = 128
    N, D = x.shape
    NB = N // P
    G = 4
    NR = NB - G
    CB = 4
    NC = NB // CB
    DEPTH = 4
    LOTS = 6
    LEFT = [3, 3, 3, 3, 4, 4] + [5] * (NB - 6)
    FIRST_SUM, FIRST_HIGH, FIRST_LOW = {0: (0, 1), 1: (3,)}, {0: (0, 1), 1: (2, 3)}, {1: (1,), 2: (2, 3)}
    U_ORDER = [0, 1, 2, 3, 4, 5, 6, 7, 8, 9, 11, 12, 14, 15, 10, 13]
    U_BEFORE, U_AFTER = {NB - 2: (0, 2)}, {NB - 1: (2, 6)}
    U_DONE = 6
    U_VECTOR = (6, 8, 10)
    PANEL1_AFTER = 13
    LATE = 4
    EPS = 1e-5
    TINY = 1e-30
    F = 4

    S = 32
    NS = P // S
    NT = NB // NS
    SPAN = N // NS

    a_rows_strips = adj.rearrange("(m u q) (s c) -> m s q u c", u=NS, q=S, c=SPAN)
    a_cols_strips = adj.rearrange("(s t b) (m c) -> m s b t c", s=NS, b=S, c=P)
    a_rows = adj.rearrange("(b p) n -> b p n", p=P)
    a_cols = adj.rearrange("(k p) (m c) -> m p k c", p=P, c=P)
    x_rows = x.rearrange("(b p) d -> b p d", p=P)
    out_rows = out.rearrange("(b p) d -> b p d", p=P)

    ctx = ExitStack()
    with ctx:
        place = [16640]

        def at(name, shape, dt, offset):
            return nc.alloc_sbuf_tensor_at(name, shape, dt, offset=offset)

        def sb(name, shape, dt):
            size = F
            for n in shape[1:]:
                size *= n
            offset = place[0]
            place[0] += -(-size // 32) * 32
            return at(name, shape, dt, offset), offset

        def sem(name):
            return ctx.enter_context(nc.semaphore(name))

        u_hi, u_hi_at = sb("u_hi", [P, NB, D], F32R)
        u_lo, u_lo_at = sb("u_lo", [P, NB, D], F32R)
        u_raw = at("u_raw", [P, NB, D], F32, u_lo_at)
        UT = NB // 2
        un = at("un", [P, 2, D], F32, u_hi_at + UT * D * F)
        un_lo = at("un_lo", [P, 3, D], F32R, u_hi_at + (UT + 2) * D * F)
        un_hi = at("un_hi", [P, 3, D], F32R, u_hi_at + (UT + 5) * D * F)
        z, z_at = sb("z", [P, 2, NB, D], F32R)
        z_hi, z_lo = z[:, 0], z[:, 1]
        z_hi_at, z_lo_at = z_at, z_at + NB * D * F
        w0_hi = at("w0_hi", [P, LOTS, G, P], F32R, z_hi_at)
        w0_lo = at("w0_lo", [P, LOTS, G, P], F32R, z_lo_at)
        x_slots = [at(f"x_slots{h}", [P, 2, D], F32, where + LOTS * G * P * F) for h, where in
                   enumerate((z_hi_at, z_lo_at))]
        x_in = [x_slots[h][:, n] for h in range(2) for n in range(2)]
        rows_x = at("rows_x", [P, DEPTH - 2, NB, P], F32, z_hi_at + NB // 2 * D * F)
        cols_x = at("cols_x", [P, DEPTH - 2, NB, P], F32, z_lo_at + NB // 2 * D * F)
        w_hi, w_hi_at = sb("w_hi", [P, 2, NB, P], F32R)
        w_lo, w_lo_at = sb("w_lo", [P, 2, NB, P], F32R)
        at_first = at("at_first", [P, NB, P], F32, w_lo_at + NB * P * F)
        junk = at("junk", [P, 2, NB, P], BF16, w_hi_at + NB * P * F)
        rows, _ = sb("rows", [P, 2, NB, P], F32)
        cols, _ = sb("cols", [P, 2, NB, P], F32)
        row_strips = [rows[:, h].rearrange("p b c -> p (b c)").rearrange("p (u c) -> p u c", c=SPAN) for h in range(2)]
        col_acc, col_acc_at = sb("col_acc", [P, NB, P], F32)
        z_raw = at("z_raw", [P, 2, 2, D], F32R, col_acc_at)
        x_res = at("x_res", [P, 2, D], F32, col_acc_at)
        y_out = at("y_out", [P, 2, D], F32, col_acc_at + 2 * D * F)
        ident, _ = sb("ident", [P, P], F32)
        ident2, _ = sb("ident2", [P, P], F32)
        ones, _ = sb("ones", [P, 1], F32)
        mhalf, _ = sb("mhalf", [P, 1], F32)
        row_sum, _ = sb("row_sum", [P, 2, NB], F32)
        deg_part, _ = sb("deg_part", [P, NB], F32)
        deg, _ = sb("deg", [P, NB], F32)
        deg_pos, _ = sb("deg_pos", [P, NB], F32)
        deg_safe, _ = sb("deg_safe", [P, NB], F32)
        deg_pow, _ = sb("deg_pow", [P, NB], F32)
        dinv, _ = sb("dinv", [P, NB], F32)
        dinv_half, _ = sb("dinv_half", [P, NB], F32)
        stats, _ = sb("stats", [P, 2, 6], F32)
        mean_var, _ = sb("mean_var", [P, 2, 2], F32)
        var_eps, _ = sb("var_eps", [P, 2], F32)
        rstd, _ = sb("rstd", [P, 2], F32)

        ps = ctx.enter_context(nc.psum_tensor("ps", [P, 8, CB * P], F32))
        acc0 = [ps[:, m] for m in range(G)]
        tp = [ps[:, n].rearrange("p (b c) -> p b c", c=P) for n in (G, G + 1)]
        csum = ps[:, G + 2]
        acc = [ps[:, G + 3], ps[:, G + 2]]

        s_const = sem("constants_made")
        s_ident = sem("ident_made")
        s_rx = [sem(f"row_and_x_loaded{s}") for s in range(4)]
        s_c = [sem(f"col_part_loaded{s}") for s in range(4)]
        s_r0 = [sem(f"row0_half_loaded{h}") for h in range(2)]
        s_c0 = [sem(f"col0_half_loaded{h}") for h in range(2)]
        s_x0 = sem("x0_loaded")
        s_t0 = sem("g0_transposed")
        s_diag0 = sem("g0_diag_added")
        s_add0 = sem("g0_chunk_added")
        s_hi0 = sem("g0_hi_ready")
        s_lo0 = sem("g0_lo_ready")
        s_hiw = sem("g0_mirror_hi_ready")
        s_rsum = sem("row_summed")
        s_cnext = sem("col_acc_next_made")
        s_cmid = sem("col_acc_near_made")
        s_cacc = sem("col_acc_made")
        s_ones = sem("col_sum_in_psum")
        s_dpart = sem("deg_part_made")
        s_deg = sem("deg_made")
        s_safe = sem("deg_safe_made")
        s_pos = sem("deg_pos_made")
        s_pow = sem("deg_pow_made")
        s_dinv = sem("dinv_made")
        s_dhalf = sem("dinv_half_made")
        s_uh = sem("u_hi_ready")
        s_ul = sem("u_lo_ready")
        s_prod = sem("g0_step_done")
        s_used = sem("g0_u_used")
        s_row = sem("row_loaded")
        s_col = [sem(f"col_loaded{s}") for s in range(2)]
        s_row2 = [sem(f"row_loaded_again{s}") for s in range(2)]
        s_xres = [sem(f"xres_loaded{s}") for s in range(2)]
        s_out = [sem(f"out_stored{s}") for s in range(2)]
        s_un = sem("u_made")
        s_ustrip = [sem(f"u_in_strips{s}") for s in range(2)]
        s_uhs = sem("u_strips_hi_ready")
        s_uls = sem("u_strips_lo_ready")
        s_ulv = sem("u_strips_lo_ready_v")
        s_zstrip = [sem(f"z_in_strips{s}") for s in range(2)]
        s_at = sem("at_made")
        s_tr = sem("row0_transposed")
        s_evac = sem("row0_copied")
        s_diag = sem("diag_added")
        s_w = sem("w_summed")
        s_hi = sem("hi_ready")
        s_lo = sem("lo_ready")
        s_mm = sem("panel_done")
        s_zh = sem("z_hi_ready")
        s_zl = sem("z_lo_ready")
        s_zlast = sem("z_lo_of_last_ready")
        s_res = sem("residual_added")
        s_stat = sem("stats_made")
        s_var = sem("var_made")
        s_veps = sem("var_eps_made")
        s_rstd = sem("rstd_made")
        s_y = sem("y_normalised")

        block = ctx.enter_context(nc.Block())

        def piece(t, k, b0, b1):
            slot, shift = k % DEPTH, 0
            if k >= NB - DEPTH:
                slot, shift = 2 + k % 2, k - DEPTH * ((k - NB + DEPTH) // 2)
            of = ((rows, cols), (rows_x, cols_x))[slot // 2][t]
            return of[:, slot % 2, b0 - shift:b1 - shift, :]

        def chunks_of(k):
            return [(b, min(b + CB, NB)) for b in range(k, NB, CB)]

        def mirrored(k):
            return NR <= k < NB - 1

        def chunk_at(k):
            return sum(len(chunks_of(j)) + mirrored(j) for j in range(k))

        def chunk_end(k):
            return chunk_at(k) + len(chunks_of(k))

        def row_x_count(k):
            return 32 * (k // 4 + (k % 4 > 0))

        def col_count(k):
            return 16 * (k // 4 + (k % 4 > 0))

        def pieces_of(k):
            cs = chunks_of(k)
            if len(cs) == 1:
                return [(k, NB, chunk_end(k))]
            first = (len(cs) + 1) // 2
            return [(k, cs[first - 1][1], chunk_at(k) + first), (cs[first][0], NB, chunk_end(k))]

        def pieces_end(k):
            return sum(len(pieces_of(j)) for j in range(k + 1))

        HALF = NB // 2

        @block.sync
        def _(sp):
            def load_first():
                for h in range(2):
                    sp.dma_start(rows[:, 0, HALF * h:HALF * h + HALF].rearrange("p b c -> p (b c)"),
                                 a_rows[0, :, HALF * h * P:(HALF * h + HALF) * P]).then_inc(s_r0[h], 16)
                for h in range(2):
                    b = max(1, HALF * h)
                    sp.dma_start(piece(1, 0, b, HALF * h + HALF), a_cols[0, :, b:HALF * h + HALF]).then_inc(s_c0[h], 16)
                sp.dma_start(x_in[0], x_rows[0]).then_inc(s_x0, 16)

            def load_step(k):
                if k >= DEPTH:
                    sp.wait_ge(s_t0, chunk_end(k - DEPTH))
                if DEPTH <= k < NB - DEPTH:
                    sp.wait_ge(s_rsum, pieces_end(k - DEPTH))
                    sp.wait_ge(s_cacc, k - DEPTH + 1)
                    sp.wait_ge(s_lo0, k - DEPTH + 1)
                sp.dma_start(piece(0, k, k, NB).rearrange("p b c -> p (b c)"),
                             a_rows[k, :, k * P:N]).then_inc(s_rx[k % 4], 16)
                if k == DEPTH:
                    sp.wait_ge(s_lo, NC)
                if k < NB - 1:
                    sp.dma_start(piece(1, k, k + 1, NB), a_cols[k, :, k + 1:NB]).then_inc(s_c[k % 4], 16)
                if k >= 4:
                    sp.wait_ge(s_ul, k - 3)
                    sp.wait_ge(s_un, k - 3)
                sp.dma_start(x_in[k % 4], x_rows[k]).then_inc(s_rx[k % 4], 16)

            def place_of(k):
                return S * (k // NT), NS * (k % NT)

            def u_to_strips(k):
                part, tile = place_of(k)
                sp.wait_ge(s_un, k + 1)
                for a in range(NS):
                    sp.dma_start(u_raw[part:part + S, tile + a],
                                 un[S * a:S * a + S, k % 2]).then_inc(s_ustrip[k % 2], 16)

            def z_to_strips(n, m):
                part, tile = place_of(m)
                if m < NR:
                    sp.wait_ge(s_zl, m + 1)
                else:
                    sp.wait_ge(s_zlast, m - NR + 1)
                for a in range(NS):
                    sp.dma_start(z[part:part + S, :, tile + a].bitcast(F32),
                                 z_raw[S * a:S * a + S, n % 2].bitcast(F32)).then_inc(s_zstrip[n % 2], 16)

            def load_row_strips(m, slot, signal):
                for s in range(NS):
                    sp.dma_start(row_strips[slot][S * s:S * s + S], a_rows_strips[m, s]).then_inc(signal, 16)

            def load_col_strips(p):
                for s in range(NS):
                    sp.dma_start(cols[S * s:S * s + S, p % 2], a_cols_strips[p, s]).then_inc(s_col[p % 2], 16)

            def slot_free(k):
                sp.wait_ge(s_t0, chunk_end(k))
                sp.wait_ge(s_rsum, pieces_end(k))
                sp.wait_ge(s_cacc, k + 1)
                sp.wait_ge(s_lo0, k + 1)

            load_first()
            for k in range(1, NB):
                if k >= LATE:
                    u_to_strips(k - LATE)
                load_step(k)
                if k == PANEL1_AFTER:
                    slot_free(NB - 2 * DEPTH)
                    load_row_strips(1, 0, s_row)
                    slot_free(NB - 2 * DEPTH + 1)
                    load_col_strips(1)
                elif k == PANEL1_AFTER + 1:
                    load_col_strips(2)
            for k in range(NB - LATE, NB):
                u_to_strips(k)
            sp.wait_ge(s_at, NC)
            load_row_strips(2, 0, s_row)

            made = [0, NR, NR + 1, 1, 2, NR + 2, NR + 3] + list(range(3, NR))

            def next_row(p):
                sp.wait_ge(s_at, NC * p)
                load_row_strips(p + 1, 0, s_row)

            def next_col(p):
                sp.wait_ge(s_lo, NC * p + NC)
                load_col_strips(p + 2)

            next_col(1)
            next_row(2)
            for n in range(3):
                z_to_strips(n, made[n])
            next_col(2)
            z_to_strips(3, made[3])
            next_row(3)
            z_to_strips(4, made[4])
            next_col(3)
            z_to_strips(5, made[5])
            next_row(4)
            z_to_strips(6, made[6])
            next_col(4)
            z_to_strips(7, made[7])
            for p in range(5, NR - 1):
                next_row(p)
                if p < NR - 2:
                    next_col(p)
                z_to_strips(p + G - 1, p - 1)
            sp.wait_ge(s_at, NC * (NR - 1))
            load_row_strips(0, 0, s_row2[0])
            sp.wait_ge(s_w, NC * NR)
            load_row_strips(1, 1, s_row2[1])
            z_to_strips(NB - 2, NR - 2)
            z_to_strips(NB - 1, NR - 1)
            sp.wait_ge(s_zstrip[0], 64 * (NB // 2))
            for j in range(2):
                sp.dma_start(x_res[:, j], x_rows[j]).then_inc(s_xres[j], 16)

            def next_panel(q, j):
                sp.wait_ge(s_at, NC * (NR + q))
                load_row_strips(q + 2, j, s_row2[j])
                sp.wait_ge(s_res, q + 1)
                sp.dma_start(x_res[:, j], x_rows[q + 2]).then_inc(s_xres[j], 16)
                store(q, j)

            def store(q, j):
                sp.wait_ge(s_y, q + 1)
                sp.dma_start(out_rows[q], y_out[:, j]).then_inc(s_out[j], 16)

            with sp.Fori(0, NB // 2 - 1) as i:
                for j in range(2):
                    next_panel(2 * i + j, j)
            for j in range(2):
                store(NB - 2 + j, j)
            for j in range(2):
                sp.wait_ge(s_out[j], 16 * (NB // 2))

        @block.gpsimd
        def _(pool):
            nc.gpsimd.memset(ones[:], 1.0).then_inc(s_const, 1)
            nc.gpsimd.memset(ident[:], 0.0).then_inc(s_const, 1)
            nc.gpsimd.memset(ident2[:], 0.0).then_inc(s_const, 1)
            nc.gpsimd.memset(mhalf[:], -0.5).then_inc(s_const, 1)
            nc.gpsimd.memset(col_acc[:], 0.0).then_inc(s_const, 1)
            pool.wait_ge(s_const, 5)
            for t, v in ((ident, 1.0), (ident2, 2.0)):
                nc.gpsimd.affine_select(out=t[:], in_=t[:], compare_op=ALU.not_equal, fill=v, base=0,
                                        pattern=[[-1, P]], channel_multiplier=1).then_inc(s_ident, 1)

            def invert_root(k):
                pool.wait_ge(s_safe, k + 1)
                nc.gpsimd.tensor_tensor(deg_pow[:, k:k + 1], deg_safe[:, k:k + 1], mhalf[:],
                                        ALU.pow).then_inc(s_pow, 1)
                pool.wait_ge(s_pow, k + 1)
                pool.wait_ge(s_pos, k + 1)
                nc.gpsimd.tensor_tensor(dinv[:, k:k + 1], deg_pow[:, k:k + 1], deg_pos[:, k:k + 1],
                                        ALU.mult).then_inc(s_dinv, 1)

            def accumulate(k, b0, b1, chunks, signal):
                pool.wait_ge(s_add0, chunks)
                return nc.gpsimd.tensor_tensor(col_acc[:, b0:b1], col_acc[:, b0:b1], piece(0, k, b0, b1),
                                               ALU.add).then_inc(signal, 1)

            def u_low_strips(n):
                t = U_ORDER[n]
                pool.wait_ge(s_uhs, n + 1)
                nc.gpsimd.tensor_tensor(u_lo[:, t], u_raw[:, t], u_hi[:, t], ALU.subtract).then_inc(s_uls, 1)

            def add_identity(p):
                s, tile = p // NT, NS * (p % NT)
                pool.wait_ge(s_col[p % 2], 64 * ((p + 1) // 2))
                for a in range(NS):
                    diag = cols[:, p % 2, tile + a, S * a:S * a + S]
                    last = nc.gpsimd.tensor_tensor(diag, diag, ident2[:, S * s:S * s + S], ALU.add)
                last.then_inc(s_diag, 1)

            for k in range(NB):
                n = chunk_at(k)
                b = k + 2
                if k < NB - 1:
                    if k >= 1:
                        pool.wait_ge(s_cacc, k)
                    accumulate(k, k + 1, b, n + 1, s_cnext)
                if len(chunks_of(k)) > 2:
                    b = k + 2 * CB
                    accumulate(k, k + 2, b, n + 2, s_cmid)
                invert_root(k)
                if b < NB:
                    accumulate(k, b, NB, chunk_end(k), s_cacc)
                if k == NR + 1:
                    add_identity(1)
                if k == NB - 2:
                    for n in range(2):
                        u_low_strips(n)

            for n in range(2, NB):
                if n not in U_VECTOR:
                    u_low_strips(n)
                if n == UT:
                    add_identity(2)
            for p in range(3, NR):
                add_identity(p)

            def rstd_of(q, j):
                pool.wait_ge(s_veps, q + 1)
                nc.gpsimd.tensor_tensor(rstd[:, j:j + 1], var_eps[:, j:j + 1], mhalf[:], ALU.pow).then_inc(s_rstd, 1)

            with pool.Fori(0, NB // 2) as i:
                for j in range(2):
                    rstd_of(2 * i + j, j)

        @block.tensor
        def _(pe):
            def passes(out_, hi, lo, mov_hi, mov_lo, first, last):
                nc.tensor.matmul(out_, hi, mov_hi, start=first, stop=False)
                nc.tensor.matmul(out_, hi, mov_lo, start=False, stop=False)
                return nc.tensor.matmul(out_, lo, mov_hi, start=False, stop=last)

            def transposes(bank, src, s):
                for b in range(src.shape[1]):
                    last = nc.tensor.transpose(tp[bank][:, b], src[:, b], ident[:])
                last.then_inc(s, 1)

            def transpose_chunk(k, n, b0, b1):
                if n < 2:
                    pe.wait_ge(s_evac, n + NC - 1)
                else:
                    pe.wait_ge(s_add0, n - 1)
                if k == 0:
                    pe.wait_ge(s_c0[(b1 - 1) // HALF], 16)
                elif b0 == k:
                    pe.wait_ge(s_rx[k % 4], row_x_count(k))
                    if k < NB - 1:
                        pe.wait_ge(s_c[k % 4], col_count(k))
                for b in range(b0, b1):
                    src = piece(0 if b == k else 1, k, b, b + 1)[:, 0]
                    last = nc.tensor.transpose(tp[n % 2][:, b - b0], src, ident[:])
                last.then_inc(s_t0, 1)

            def mirror_step(k):
                n = chunk_end(k)
                pe.wait_ge(s_add0, n)
                transposes(n % 2, piece(0, k, k + 1, NB), s_t0)

            def col_sums(k):
                pe.wait_ge(s_cnext, k)
                pe.wait_ge(s_deg, k)
                nc.tensor.matmul(csum[:, k:k + 1], col_acc[:, k], ones[:], start=True, stop=True).then_inc(s_ones, 1)

            def multiply0(k, m):
                if m == 0:
                    pe.wait_ge(s_ul, k + 1)
                    pe.wait_ge(s_lo0, k + 1)
                    if k > NR:
                        pe.wait_ge(s_add0, chunk_end(k - 1) + 1)
                if m < G:
                    last = passes(acc0[m], w0_hi[:, k % LOTS, m], w0_lo[:, k % LOTS, m],
                                  un_hi[:, k % 3], un_lo[:, k % 3],
                                  k == 0, k == NB - 1)
                    if m == G - 1:
                        last.then_inc(s_prod, 1)
                else:
                    pe.wait_ge(s_lo, k // CB + 1)
                    last = passes(acc[0], w_hi[:, 0, k], w_lo[:, 0, k], un_hi[:, k % 3], un_lo[:, k % 3],
                                  k == 0, k == NB - 1)
                    last.then_inc(s_mm if k == NB - 1 else s_used, 1)

            pe.wait_ge(s_ident, 2)
            for c in range(NC):
                pe.wait_ge(s_r0[CB * c // HALF], 16)
                if c >= 2:
                    pe.wait_ge(s_evac, c - 1)
                transposes(c % 2, rows[:, 0, CB * c:CB * c + CB], s_tr)
            done = 0
            for k in range(NB):
                if k >= 1 and mirrored(k - 1):
                    mirror_step(k - 1)
                for n, (b0, b1) in enumerate(chunks_of(k)):
                    if n >= 1 and done < (G + 1) * (k - 1):
                        multiply0(done // (G + 1), done % (G + 1))
                        done += 1
                    transpose_chunk(k, chunk_at(k) + n, b0, b1)
                    if 1 <= k < NR and n == min(1, len(chunks_of(k)) - 1):
                        col_sums(k)
                while done < (G + 1) * k - LEFT[k]:
                    if k >= NR and done == (G + 1) * k - LEFT[k] - 3:
                        col_sums(k)
                    multiply0(done // (G + 1), done % (G + 1))
                    done += 1
            while done < (G + 1) * NB:
                multiply0(done // (G + 1), done % (G + 1))
                done += 1

            def multiply(g, j, mov_hi, mov_lo, tile_ready=lambda n: None, order=range(NB)):
                chunks = 0
                for n, t in enumerate(order):
                    if t // CB >= chunks:
                        chunks = t // CB + 1
                        pe.wait_ge(s_lo, NC * g + chunks)
                    tile_ready(n)
                    last = passes(acc[j], w_hi[:, j, t], w_lo[:, j, t], mov_hi[:, t], mov_lo[:, t],
                                  n == 0, n == NB - 1)
                last.then_inc(s_mm, 1)

            def u_ready(n):
                by_vector = sum(m <= n for m in U_VECTOR)
                if n in U_VECTOR:
                    pe.wait_ge(s_ulv, by_vector)
                else:
                    pe.wait_ge(s_uls, n + 1 - by_vector)

            multiply(1, 1, u_hi, u_lo, u_ready, U_ORDER)
            with pe.Fori(0, NR // 2 - 1) as i:
                for j in range(2):
                    p = 2 * i + 2 + j
                    pe.wait_ge(s_zl, p - 1)
                    multiply(p, j, u_hi, u_lo)

            def z_ready(t):
                if t % NS == 0:
                    n = NB - NT + t // NS
                    for m in (n, n - 1):
                        pe.wait_ge(s_zstrip[m % 2], 64 * (m // 2 + 1))

            pe.wait_ge(s_zl, NR - 1)
            multiply(NR, 0, z_hi, z_lo, z_ready)
            pe.wait_ge(s_zl, NR)
            multiply(NR + 1, 1, z_hi, z_lo)
            with pe.Fori(1, NB // 2) as i:
                for j in range(2):
                    q = 2 * i + j
                    pe.wait_ge(s_res, q - 1)
                    multiply(NR + q, j, z_hi, z_lo)

        @block.scalar
        def _(act):
            for c in range(NC):
                act.wait_ge(s_tr, c + 1)
                nc.scalar.activation(at_first[:, CB * c:CB * c + CB], tp[c % 2], ACT.Copy).then_inc(s_evac, 1)

            def high_first(c):
                act.wait_ge(s_w, c + 1)
                nc.scalar.activation(w_hi[:, 0, CB * c:CB * c + CB], cols[:, 0, CB * c:CB * c + CB],
                                     ACT.Copy).then_inc(s_hi, 1)

            def u_high_strips(n0, n1):
                for t in U_ORDER[n0:n1]:
                    k = NB - NT + t // NS
                    for n in (k, k - 1):
                        act.wait_ge(s_ustrip[n % 2], 64 * (n // 2 + 1))
                    if t >= UT:
                        act.wait_ge(s_ustrip[1], 64 * (NB // 2))
                        if t >= UT + 2:
                            last = max(k for k in range(NB) if k % 3 == (t - UT - 2) % 3)
                            if last == NB - 1:
                                act.wait_ge(s_prod, NB)
                                act.wait_ge(s_mm, 1)
                            else:
                                act.wait_ge(s_used, last + 1)
                    nc.scalar.activation(u_hi[:, t], u_raw[:, t], ACT.Copy).then_inc(s_uhs, 1)

            def high1_chunk(p, j, c):
                act.wait_ge(s_w, NC * p + c + 1)
                nc.scalar.activation(w_hi[:, j, CB * c:CB * c + CB], cols[:, j, CB * c:CB * c + CB],
                                     ACT.Copy).then_inc(s_hi, 1)

            def high1(p, j):
                for c in range(NC):
                    high1_chunk(p, j, c)

            for k in range(NB):
                if k >= 1 and mirrored(k - 1):
                    j = k - 1
                    act.wait_ge(s_t0, chunk_end(j) + 1)
                    act.wait_ge(s_prod, NB - LOTS)
                    nc.scalar.activation(w0_hi[:, k % LOTS:k % LOTS + NB - k, j - NR],
                                         tp[chunk_end(j) % 2][:, 0:NB - k], ACT.Copy).then_inc(s_hiw, 1)
                if k >= 2:
                    act.wait_ge(s_rsum, pieces_end(k - 2))
                for t, (b0, b1, chunks) in enumerate(pieces_of(k)):
                    if k < NR:
                        act.wait_ge(s_add0, chunks)
                    else:
                        act.wait_ge(s_diag0, k - NR + 1)
                    nc.scalar.activation(junk[:, k % 2, b0:b1], piece(0, k, b0, b1), ACT.Copy,
                                         accum_out=row_sum[:, t, k:k + 1]).then_inc(s_rsum, 1)
                if k >= LOTS:
                    act.wait_ge(s_prod, k - LOTS + 1)
                b = max(k, NR)
                nc.scalar.activation(w0_hi[:, k % LOTS, b - NR:G], piece(0, k, b, NB), ACT.Copy).then_inc(s_hi0, 1)
                u_high_strips(*U_BEFORE.get(k, (0, 0)))
                if k == NB - 1:
                    high1_chunk(1, 1, 0)
                if k == 0:
                    act.wait_ge(s_x0, 16)
                act.wait_ge(s_dinv, k + 1)
                if k >= 3:
                    act.wait_ge(s_used, k - 2)
                nc.scalar.activation(un_hi[:, k % 3], x_in[k % 4], ACT.Copy, scale=dinv[:, k:k + 1]).then_inc(s_uh, 1)
                if k >= 2:
                    act.wait_ge(s_ustrip[k % 2], 64 * (k // 2))
                nc.scalar.activation(un[:, k % 2], x_in[k % 4], ACT.Copy, scale=dinv[:, k:k + 1]).then_inc(s_un, 1)
                u_high_strips(*U_AFTER.get(k, (0, 0)))
                for c in FIRST_HIGH.get(k, ()):
                    high_first(c)

            def z_high(n, m, src, j):
                if n >= 2:
                    act.wait_ge(s_zstrip[j], 64 * (n // 2))
                nc.scalar.activation(z_raw[:, j, 0], src, ACT.Copy, scale=dinv_half[:, m:m + 1]).then_inc(s_zh, 1)

            def z_after(p, i, j):
                act.wait_ge(s_mm, p + 1)
                act.wait_ge(s_zstrip[j], 64 * (i + G // 2))
                nc.scalar.activation(z_raw[:, j, 0], acc[j], ACT.Copy,
                                     scale=dinv_half[:, bass.ds(p, 1)]).then_inc(s_zh, 1)

            u_high_strips(U_DONE, UT)
            for c in range(1, NC):
                high1_chunk(1, 1, c)
            u_high_strips(UT, NB)
            act.wait_ge(s_prod, NB)
            act.wait_ge(s_mm, 1)
            act.wait_ge(s_dhalf, 1)
            z_high(0, 0, acc[0], 0)
            z_high(1, NR, acc0[0], 1)
            high1(2, 0)
            z_high(2, NR + 1, acc0[1], 0)
            act.wait_ge(s_mm, 2)
            z_high(3, 1, acc[1], 1)
            high1(3, 1)
            act.wait_ge(s_mm, 3)
            z_high(4, 2, acc[0], 0)
            z_high(5, NR + 2, acc0[2], 1)
            high1(4, 0)
            z_high(6, NR + 3, acc0[3], 0)
            z_after(3, 1, 1)
            with act.Fori(2, NR // 2 - 1) as i:
                for j in range(2):
                    p = 2 * i + j
                    act.wait_ge(s_mm, p)
                    high1(p + 1, 1 - j)
                    z_after(p, i, j)
            act.wait_ge(s_mm, NR - 2)
            high1(NR - 1, 1)
            z_after(NR - 2, NR // 2 - 1, 0)

            def high2(q, j):
                act.wait_ge(s_mm, NR + q - 1)
                for c in range(NC):
                    act.wait_ge(s_at, NC * (NR - 1 + q) + c + 1)
                    nc.scalar.activation(w_hi[:, j, CB * c:CB * c + CB], cols[:, j, CB * c:CB * c + CB],
                                         ACT.Copy).then_inc(s_hi, 1)

            high2(0, 0)
            z_after(NR - 1, NR // 2 - 1, 1)
            high2(1, 1)
            with act.Fori(1, NB // 2) as i:
                for j in range(2):
                    high2(2 * i + j, j)

        @block.vector
        def _(dve):
            dve.wait_ge(s_ident, 2)

            def add(out_, a, b, s):
                return nc.vector.tensor_tensor(out_, a, b, ALU.add).then_inc(s, 1)

            def degrees(k):
                two = len(pieces_of(k)) == 2
                made, signal = (deg_part, s_dpart) if two else (deg, s_deg)
                dve.wait_ge(s_rsum, pieces_end(k) - two)
                if k == 0:
                    nc.vector.tensor_scalar(made[:, 0:1], row_sum[:, 0, 0:1], 0.5, None, ALU.mult).then_inc(signal, 1)
                else:
                    dve.wait_ge(s_ones, k)
                    nc.vector.tensor_scalar(made[:, k:k + 1], csum[:, k:k + 1], row_sum[:, 0, k:k + 1], 0.5, ALU.add,
                                            ALU.mult).then_inc(signal, 1)
                if two:
                    dve.wait_ge(s_rsum, pieces_end(k))
                    dve.wait_ge(s_dpart, k + 1)
                    nc.vector.tensor_scalar(deg[:, k:k + 1], row_sum[:, 1, k:k + 1], 0.5, deg_part[:, k:k + 1],
                                            ALU.mult, ALU.add).then_inc(s_deg, 1)
                dve.wait_ge(s_deg, k + 1)
                one = 1.0 if k < NR else 0.0
                nc.vector.tensor_scalar(deg_safe[:, k:k + 1], deg[:, k:k + 1], one, TINY, ALU.add,
                                        ALU.max).then_inc(s_safe, 1)
                nc.vector.tensor_scalar(deg_pos[:, k:k + 1], deg[:, k:k + 1], -one, None, ALU.is_gt).then_inc(s_pos, 1)

            def u_low(k):
                dve.wait_ge(s_uh, k + 1)
                nc.vector.scalar_tensor_tensor(un_lo[:, k % 3], x_in[k % 4], dinv[:, k:k + 1], un_hi[:, k % 3],
                                               ALU.mult, ALU.subtract).then_inc(s_ul, 1)

            def low(g, j, c, src):
                dve.wait_ge(s_hi, NC * g + c + 1)
                nc.vector.tensor_tensor(w_lo[:, j, CB * c:CB * c + CB], src, w_hi[:, j, CB * c:CB * c + CB],
                                        ALU.subtract).then_inc(s_lo, 1)

            def transpose_chunk(c, source, target):
                nc.vector.transpose(target[:, CB * c:CB * c + CB].rearrange("p t (u q) -> p u t q", q=S),
                                    source[:, :, P * c:P * c + P].rearrange("p u (t q) -> p u t q", q=S)
                                    ).then_inc(s_at, 1)

            def sum_chunk(p, j, c):
                dve.wait_ge(s_at, NC * (p - 1) + c + 1)
                add(cols[:, j, CB * c:CB * c + CB], rows[:, 1, CB * c:CB * c + CB],
                    cols[:, j, CB * c:CB * c + CB], s_w)

            def low_chunk(p, j, c):
                low(p, j, c, cols[:, j, CB * c:CB * c + CB])

            def begin1(p):
                dve.wait_ge(s_row, 64 * p)
                dve.wait_ge(s_w, NC * p)
                transpose_chunk(0, row_strips[0], rows[:, 1])
                transpose_chunk(1, row_strips[0], rows[:, 1])

            def sums1(p, j):
                dve.wait_ge(s_diag, p + 1)
                sum_chunk(p, j, 0)
                transpose_chunk(2, row_strips[0], rows[:, 1])
                sum_chunk(p, j, 1)

            def more_sums1(p, j):
                transpose_chunk(3, row_strips[0], rows[:, 1])
                sum_chunk(p, j, 2)
                sum_chunk(p, j, 3)

            def end1(p, j):
                low_chunk(p, j, 0)
                more_sums1(p, j)
                for c in range(1, NC):
                    low_chunk(p, j, c)

            def panel1(p, j):
                begin1(p)
                sums1(p, j)
                end1(p, j)

            def sum_first(c):
                b = CB * c
                if c == 0:
                    dve.wait_ge(s_add0, 1)
                    add(cols[:, 0, 0], rows[:, 0, 0], ident2[:], s_diag)
                    b = 1
                dve.wait_ge(s_evac, c + 1)
                add(cols[:, 0, b:CB * c + CB], at_first[:, b:CB * c + CB], cols[:, 0, b:CB * c + CB], s_w)

            for k in range(NB):
                if k >= 1 and mirrored(k - 1):
                    dve.wait_ge(s_hiw, k - NR)
                    lots = slice(k % LOTS, k % LOTS + NB - k)
                    nc.vector.tensor_tensor(w0_lo[:, lots, k - 1 - NR], tp[chunk_end(k - 1) % 2][:, 0:NB - k],
                                            w0_hi[:, lots, k - 1 - NR], ALU.subtract).then_inc(s_add0, 1)
                if k == 1:
                    dve.wait_ge(s_x0, 16)
                    u_low(0)
                    low(0, 0, 0, cols[:, 0, 0:CB])
                if k >= 1:
                    dve.wait_ge(s_rx[k % 4], row_x_count(k))
                n = chunk_at(k)
                for t, (b0, b1) in enumerate(chunks_of(k)):
                    dve.wait_ge(s_t0, n + 1)
                    w = piece(0, k, b0, b1)
                    add(w, tp[n % 2][:, 0:b1 - b0], w, s_add0)
                    n += 1
                    if k >= 2 and t == min(1, len(chunks_of(k)) - 1):
                        u_low(k - 1)
                if k >= NR:
                    diag = piece(0, k, k, k + 1)[:, 0]
                    dve.wait_ge(s_add0, n)
                    add(diag, diag, ident2[:], s_diag0)
                for c in FIRST_LOW.get(k, ()):
                    low(0, 0, c, cols[:, 0, CB * c:CB * c + CB])
                for c in FIRST_SUM.get(k, ()):
                    sum_first(c)
                degrees(k)
                if k == 0:
                    sum_first(2)
                b = max(k, NR)
                dve.wait_ge(s_hi0, k + 1)
                nc.vector.tensor_tensor(w0_lo[:, k % LOTS, b - NR:G], piece(0, k, b, NB),
                                        w0_hi[:, k % LOTS, b - NR:G], ALU.subtract).then_inc(s_lo0, 1)
                if k == NB - 3:
                    dve.wait_ge(s_col[1], 64)
                    begin1(1)
                elif k == NB - 2:
                    sums1(1, 1)
                elif k == NB - 1:
                    more_sums1(1, 1)
                    low_chunk(1, 1, 0)
            u_low(NB - 1)
            dve.wait_ge(s_dinv, NB)
            nc.vector.tensor_scalar(dinv_half[:], dinv[:], 0.5, None, ALU.mult).then_inc(s_dhalf, 1)

            def z_low(n, m, src, j, signal=s_zl):
                dve.wait_ge(s_zh, n + 1)
                nc.vector.scalar_tensor_tensor(z_raw[:, j, 1], src, dinv_half[:, bass.ds(m, 1)], z_raw[:, j, 0],
                                               ALU.mult, ALU.subtract).then_inc(signal, 1)

            for c in range(1, NC):
                low_chunk(1, 1, c)
            for n in U_VECTOR:
                t = U_ORDER[n]
                dve.wait_ge(s_uhs, n + 1)
                nc.vector.tensor_tensor(u_lo[:, t], u_raw[:, t], u_hi[:, t], ALU.subtract).then_inc(s_ulv, 1)
            begin1(2)
            sums1(2, 0)
            z_low(0, 0, acc[0], 0)
            z_low(1, NR, acc0[0], 1, s_zlast)
            end1(2, 0)
            z_low(2, NR + 1, acc0[1], 0, s_zlast)
            begin1(3)
            sums1(3, 1)
            z_low(3, 1, acc[1], 1)
            end1(3, 1)
            z_low(4, 2, acc[0], 0)
            begin1(4)
            sums1(4, 0)
            z_low(5, NR + 2, acc0[2], 1, s_zlast)
            end1(4, 0)
            z_low(6, NR + 3, acc0[3], 0, s_zlast)
            z_low(7, 3, acc[1], 1)
            with dve.Fori(2, NR // 2 - 1) as i:
                for j in range(2):
                    p = 2 * i + j
                    panel1(p + 1, 1 - j)
                    z_low(G + p, p, acc[j], j)
            panel1(NR - 1, 1)
            z_low(NB - 2, NR - 2, acc[0], 0)

            def panel2(q, i, j):
                def low_chunk(c):
                    low(NR + q, j, c, cols[:, j, CB * c:CB * c + CB])

                dve.wait_ge(s_row2[j], 64 * i + 64)
                dve.wait_ge(s_lo, NC * (NR + q - 1))
                transpose_chunk(0, row_strips[j], cols[:, j])
                for c in range(1, NC):
                    transpose_chunk(c, row_strips[j], cols[:, j])
                    low_chunk(c - 1)
                low_chunk(NC - 1)

            def finish(q, i, j, again):
                dve.wait_ge(s_xres[j], 16 * i + 16)
                if again:
                    dve.wait_ge(s_out[j], 16 * i)
                dve.wait_ge(s_mm, NR + q + 1)
                add(y_out[:, j], acc[j], x_res[:, j], s_res)
                dve.wait_ge(s_res, q + 1)
                nc.vector.bn_stats(stats[:, j], y_out[:, j]).then_inc(s_stat, 1)
                dve.wait_ge(s_ident, 2)
                dve.wait_ge(s_stat, q + 1)
                nc.vector.bn_aggr(mean_var[:, j], stats[:, j]).then_inc(s_var, 1)
                dve.wait_ge(s_var, q + 1)
                nc.vector.tensor_scalar(var_eps[:, j:j + 1], mean_var[:, j, 1:2], EPS, None,
                                        ALU.add).then_inc(s_veps, 1)
                dve.wait_ge(s_rstd, q + 1)
                nc.vector.tensor_scalar(y_out[:, j], y_out[:, j], mean_var[:, j, 0:1], rstd[:, j:j + 1],
                                        ALU.subtract, ALU.mult).then_inc(s_y, 1)

            panel2(0, 0, 0)
            z_low(NB - 1, NR - 1, acc[1], 1)
            panel2(1, 0, 1)
            finish(0, 0, 0, False)
            panel2(2, 1, 0)
            finish(1, 0, 1, False)
            with dve.Fori(1, NB // 2 - 1) as i:
                for j in range(2):
                    q = 2 * i + j
                    panel2(q + 1, i + j, 1 - j)
                    finish(q, i, j, True)
            panel2(NB - 1, NB // 2 - 1, 1)
            finish(NB - 2, NB // 2 - 1, 0, True)
            finish(NB - 1, NB // 2 - 1, 1, True)


def kernel(x, adj):
    import numpy as np

    import concourse.bacc as bacc
    from concourse import mybir
    from concourse.bass_utils import run_bass_kernel_spmd

    nc = bacc.Bacc("TRN2", target_bir_lowering=False, num_devices=1)
    arrays = {"x": np.ascontiguousarray(x), "adj": np.ascontiguousarray(adj)}
    aps = [nc.dram_tensor(n, a.shape, mybir.dt.float32, kind="ExternalInput").ap() for n, a in arrays.items()]
    out = nc.dram_tensor("out", arrays["x"].shape, mybir.dt.float32, kind="ExternalOutput").ap()
    build(nc, *aps, out)
    return run_bass_kernel_spmd(nc, [arrays], core_ids=[0]).results[0]["out"]
```
